# Optimizing a Trainium2 kernel written in Bass

```python
import numpy as np
import jax
import jax.numpy as jnp

def _softmax(x, axis=-1):
    return jax.nn.softmax(x, axis=axis)

def _gelu(x):
    return jax.nn.gelu(x, approximate=True)

def _silu(x):
    return jax.nn.silu(x)

def _sigmoid(x):
    return jax.nn.sigmoid(x)

def _layernorm(x, axis=-1, eps=1e-05):
    m = jnp.mean(x, axis=axis, keepdims=True)
    v = jnp.var(x, axis=axis, keepdims=True)
    return (x - m) / jnp.sqrt(v + eps)

def _scatter_add(tgt, idx, src, axis=0):
    return tgt.at[idx].add(src)

def _segment_sum(src, seg, n):
    return jax.ops.segment_sum(src, seg, n)
kernel_name = 'mk_recurrent_d2_jaxref_r8_99eb28'

def setup_inputs(seed: int=0):
    np.random.seed(seed)
    _w = jnp.asarray

    def _L0_attn_setup():
        import jax, jax.numpy as jnp
        import numpy as np
        B, S, D, H = (4, 256, 128, 16)
        HD = D // H
        LN_EPS = 1e-05
        KERN_EPS = 1e-06

        def kernel_func(q, k):
            scores = jnp.einsum('bhqd,bhkd->bhqk', q, k) / jnp.sqrt(jnp.asarray(HD, q.dtype))
            w = jax.nn.relu(scores)
            return w / (jnp.sum(w, axis=-1, keepdims=True) + KERN_EPS)
        key = jax.random.key(seed)
        k1, k2, k3 = jax.random.split(key, 3)
        scale = 1.0 / np.sqrt(D)
        return {'x': jax.random.normal(k1, (B, S, D), dtype=jnp.float32), 'w_qkv': jax.random.normal(k2, (D, 3 * D), dtype=jnp.float32) * scale, 'w_out': jax.random.normal(k3, (D, D), dtype=jnp.float32) * scale, 'b_out': jnp.zeros((D,), dtype=jnp.float32), 'gamma': jnp.ones((D,), dtype=jnp.float32), 'beta': jnp.zeros((D,), dtype=jnp.float32)}
    _L0_attn_in = _L0_attn_setup()

    def _L0_ffn_setup():
        import jax, jax.numpy as jnp
        import numpy as np
        B, S, D, H, F = (4, 512, 128, 16, 512)
        CAP = 0.125
        ROPE_BASE = 10000.0

        def rmsnorm(x, g):
            return x * jax.lax.rsqrt(jnp.mean(x * x, -1, keepdims=True) + 1e-06) * g

        def rope(t, pos):
            hd = t.shape[-1]
            inv = 1.0 / ROPE_BASE ** (jnp.arange(0, hd, 2, dtype=jnp.float32) / hd)
            f = pos[:, None, :, None].astype(jnp.float32) * inv
            emb = jnp.concatenate([f, f], axis=-1)
            cos, sin = (jnp.cos(emb), jnp.sin(emb))
            rot = jnp.concatenate([-t[..., hd // 2:], t[..., :hd // 2]], axis=-1)
            return t * cos + rot * sin
        key = jax.random.key(seed)
        ks = jax.random.split(key, 9)
        scale = 0.02
        x = jax.random.normal(ks[0], (B, S, D), jnp.float32)
        causal = jnp.where(jnp.tril(jnp.ones((S, S), bool)), 0.0, -1000000000.0).astype(jnp.float32)
        attention_mask = jnp.broadcast_to(causal[None, None], (B, 1, S, S))
        position_ids = jnp.broadcast_to(jnp.arange(S, dtype=jnp.int32), (B, S))
        return {'x': x, 'attention_mask': attention_mask, 'position_ids': position_ids, 'router_w': jax.random.normal(ks[1], (D, 1), jnp.float32) * scale, 'router_b': jnp.zeros((1,), jnp.float32), 'wq': jax.random.normal(ks[2], (D, D), jnp.float32) * scale, 'wk': jax.random.normal(ks[3], (D, D), jnp.float32) * scale, 'wv': jax.random.normal(ks[4], (D, D), jnp.float32) * scale, 'wo': jax.random.normal(ks[5], (D, D), jnp.float32) * scale, 'w1': jax.random.normal(ks[6], (D, F), jnp.float32) * scale, 'w2': jax.random.normal(ks[7], (F, D), jnp.float32) * scale, 'ln1': jnp.ones((D,), jnp.float32), 'ln2': jnp.ones((D,), jnp.float32)}
    _L0_ffn_in = _L0_ffn_setup()

    def _L1_attn_setup():
        import jax, jax.numpy as jnp
        import numpy as np
        N_HEADS, D_MODEL, D_HEAD = (16, 128, 64)
        BATCH, SEQ = (2, 256)
        INIT_RANGE = 0.02
        key = jax.random.key(seed)
        ks = jax.random.split(key, 5)
        x = jax.random.normal(ks[0], (BATCH, SEQ, D_MODEL), dtype=jnp.float32)
        W_Q = jax.random.normal(ks[1], (N_HEADS, D_MODEL, D_HEAD), dtype=jnp.float32) * INIT_RANGE
        W_K = jax.random.normal(ks[2], (N_HEADS, D_MODEL, D_HEAD), dtype=jnp.float32) * INIT_RANGE
        W_V = jax.random.normal(ks[3], (N_HEADS, D_MODEL, D_HEAD), dtype=jnp.float32) * INIT_RANGE
        W_O = jax.random.normal(ks[4], (N_HEADS, D_HEAD, D_MODEL), dtype=jnp.float32) * INIT_RANGE
        b_Q = jnp.zeros((N_HEADS, D_HEAD), dtype=jnp.float32)
        b_K = jnp.zeros((N_HEADS, D_HEAD), dtype=jnp.float32)
        b_V = jnp.zeros((N_HEADS, D_HEAD), dtype=jnp.float32)
        b_O = jnp.zeros((D_MODEL,), dtype=jnp.float32)
        return {'normalized_resid_pre': x, 'W_Q': W_Q, 'W_K': W_K, 'W_V': W_V, 'W_O': W_O, 'b_Q': b_Q, 'b_K': b_K, 'b_V': b_V, 'b_O': b_O}
    _L1_attn_in = _L1_attn_setup()

    def _L1_ffn_setup():
        import jax, jax.numpy as jnp
        import numpy as np
        DIM = 128
        HIDDEN = 384
        SCALE = 1.0 / 127.0

        def _dequant(w_int, dtype):
            return w_int.astype(dtype) * jnp.asarray(SCALE, dtype)
        key = jax.random.key(seed)
        k_x, k_g, k_u, k_d = jax.random.split(key, 4)
        x = jax.random.normal(k_x, (4, 256, DIM), dtype=jnp.float32)
        w_gate = jax.random.randint(k_g, (HIDDEN, DIM), -127, 128, dtype=jnp.int32)
        w_up = jax.random.randint(k_u, (HIDDEN, DIM), -127, 128, dtype=jnp.int32)
        w_down = jax.random.randint(k_d, (DIM, HIDDEN), -127, 128, dtype=jnp.int32)
        return {'x': x, 'w_gate': w_gate, 'w_up': w_up, 'w_down': w_down}
    _L1_ffn_in = _L1_ffn_setup()
    _d = {'L0_attn_x': _L0_attn_in['x'], 'L0_attn_w_qkv': _L0_attn_in['w_qkv'], 'L0_attn_w_out': _L0_attn_in['w_out'], 'L0_attn_b_out': _L0_attn_in['b_out'], 'L0_attn_gamma': _L0_attn_in['gamma'], 'L0_attn_beta': _L0_attn_in['beta'], 'L0_ffn_attention_mask': _L0_ffn_in['attention_mask'], 'L0_ffn_position_ids': _L0_ffn_in['position_ids'], 'L0_ffn_router_w': _L0_ffn_in['router_w'], 'L0_ffn_router_b': _L0_ffn_in['router_b'], 'L0_ffn_wq': _L0_ffn_in['wq'], 'L0_ffn_wk': _L0_ffn_in['wk'], 'L0_ffn_wv': _L0_ffn_in['wv'], 'L0_ffn_wo': _L0_ffn_in['wo'], 'L0_ffn_w1': _L0_ffn_in['w1'], 'L0_ffn_w2': _L0_ffn_in['w2'], 'L0_ffn_ln1': _L0_ffn_in['ln1'], 'L0_ffn_ln2': _L0_ffn_in['ln2'], 'L1_attn_W_Q': _L1_attn_in['W_Q'], 'L1_attn_W_K': _L1_attn_in['W_K'], 'L1_attn_W_V': _L1_attn_in['W_V'], 'L1_attn_W_O': _L1_attn_in['W_O'], 'L1_attn_b_Q': _L1_attn_in['b_Q'], 'L1_attn_b_K': _L1_attn_in['b_K'], 'L1_attn_b_V': _L1_attn_in['b_V'], 'L1_attn_b_O': _L1_attn_in['b_O'], 'L1_ffn_w_gate': _L1_ffn_in['w_gate'], 'L1_ffn_w_up': _L1_ffn_in['w_up'], 'L1_ffn_w_down': _L1_ffn_in['w_down']}
    _x0 = _d['L0_attn_x']
    _d['L0_attn_x'] = jax.random.normal(jax.random.fold_in(jax.random.key(seed), 1), (1, 2048, 128), dtype=_x0.dtype)
    del _x0
    return _d

def reference(L0_attn_x, L0_attn_w_qkv, L0_attn_w_out, L0_attn_b_out, L0_attn_gamma, L0_attn_beta, L0_ffn_attention_mask, L0_ffn_position_ids, L0_ffn_router_w, L0_ffn_router_b, L0_ffn_wq, L0_ffn_wk, L0_ffn_wv, L0_ffn_wo, L0_ffn_w1, L0_ffn_w2, L0_ffn_ln1, L0_ffn_ln2, L1_attn_W_Q, L1_attn_W_K, L1_attn_W_V, L1_attn_W_O, L1_attn_b_Q, L1_attn_b_K, L1_attn_b_V, L1_attn_b_O, L1_ffn_w_gate, L1_ffn_w_up, L1_ffn_w_down):

    def _L0_attn_ref(x, w_qkv, w_out, b_out, gamma, beta):
        import jax, jax.numpy as jnp
        import numpy as np
        B, S, D, H = (4, 256, 128, 16)
        HD = D // H
        LN_EPS = 1e-05
        KERN_EPS = 1e-06

        def kernel_func(q, k):
            scores = jnp.einsum('bhqd,bhkd->bhqk', q, k) / jnp.sqrt(jnp.asarray(HD, q.dtype))
            w = jax.nn.relu(scores)
            return w / (jnp.sum(w, axis=-1, keepdims=True) + KERN_EPS)
        Bx, Sx, _ = x.shape
        qkv = (x @ w_qkv).reshape(Bx, Sx, H, 3 * HD)
        q, k, v = jnp.split(qkv, 3, axis=-1)
        q = q.transpose(0, 2, 1, 3)
        k = k.transpose(0, 2, 1, 3)
        v = v.transpose(0, 2, 1, 3)
        attn = kernel_func(q, k)
        out = jnp.einsum('bhqk,bhkd->bhqd', attn, v)
        out = out.transpose(0, 2, 1, 3).reshape(Bx, Sx, D)
        out = out @ w_out + b_out
        y = x + out
        mu = jnp.mean(y, axis=-1, keepdims=True)
        var = jnp.var(y, axis=-1, keepdims=True)
        return (y - mu) * jax.lax.rsqrt(var + LN_EPS) * gamma + beta

    def _L0_ffn_ref(x, attention_mask, position_ids, router_w, router_b, wq, wk, wv, wo, w1, w2, ln1, ln2):
        import jax, jax.numpy as jnp
        import numpy as np
        B, S, D, H, F = (4, 512, 128, 16, 512)
        CAP = 0.125
        ROPE_BASE = 10000.0

        def rmsnorm(x, g):
            return x * jax.lax.rsqrt(jnp.mean(x * x, -1, keepdims=True) + 1e-06) * g

        def rope(t, pos):
            hd = t.shape[-1]
            inv = 1.0 / ROPE_BASE ** (jnp.arange(0, hd, 2, dtype=jnp.float32) / hd)
            f = pos[:, None, :, None].astype(jnp.float32) * inv
            emb = jnp.concatenate([f, f], axis=-1)
            cos, sin = (jnp.cos(emb), jnp.sin(emb))
            rot = jnp.concatenate([-t[..., hd // 2:], t[..., :hd // 2]], axis=-1)
            return t * cos + rot * sin
        b, s, d = x.shape
        hd = d // H
        weights = (x @ router_w)[..., 0] + router_b[0]
        k = int(CAP * s)
        topv, topi = jax.lax.top_k(weights, k)
        thr = topv[:, -1]
        sel_mask = (weights > thr[:, None]).astype(x.dtype)
        kc = k - 1
        sel_idx = jnp.sort(topi[:, :kc], axis=1)
        bidx = jnp.arange(b)[:, None]
        x_sel = x[bidx, sel_idx]
        pos_sel = position_ids[bidx, sel_idx]
        w_sel = weights[bidx, sel_idx]
        m = attention_mask[:, 0]
        m_sel = m[bidx[:, :, None], sel_idx[:, :, None], sel_idx[:, None, :]]
        hn = rmsnorm(x_sel, ln1)

        def heads(t):
            return t.reshape(b, kc, H, hd).transpose(0, 2, 1, 3)
        q = rope(heads(hn @ wq), pos_sel)
        kk = rope(heads(hn @ wk), pos_sel)
        v = heads(hn @ wv)
        sc = jnp.einsum('bhqd,bhkd->bhqk', q, kk) / np.sqrt(hd).astype(np.float32)
        sc = sc + m_sel[:, None]
        a = jax.nn.softmax(sc, axis=-1)
        o = jnp.einsum('bhqk,bhkd->bhqd', a, v).transpose(0, 2, 1, 3).reshape(b, kc, d) @ wo
        x1 = x_sel + o
        x2 = x1 + jax.nn.gelu(rmsnorm(x1, ln2) @ w1) @ w2
        proc = x2 * w_sel[..., None]
        out = jnp.zeros_like(x).at[bidx, sel_idx].set(proc)
        return out + x * (1.0 - sel_mask)[..., None]

    def _L1_attn_ref(normalized_resid_pre, W_Q, W_K, W_V, W_O, b_Q, b_K, b_V, b_O):
        import jax, jax.numpy as jnp
        import numpy as np
        N_HEADS, D_MODEL, D_HEAD = (16, 128, 64)
        BATCH, SEQ = (2, 256)
        INIT_RANGE = 0.02
        x = normalized_resid_pre
        q = jnp.einsum('bsm,hmd->bshd', x, W_Q) + b_Q
        k = jnp.einsum('bsm,hmd->bshd', x, W_K) + b_K
        v = jnp.einsum('bsm,hmd->bshd', x, W_V) + b_V
        scores = jnp.einsum('bqhd,bkhd->bhqk', q, k) / jnp.sqrt(jnp.float32(D_HEAD))
        seq = x.shape[1]
        causal = jnp.tril(jnp.ones((seq, seq), dtype=bool))
        scores = jnp.where(causal, scores, jnp.float32(-jnp.inf))
        pattern = jax.nn.softmax(scores, axis=-1)
        z = jnp.einsum('bhqk,bkhd->bqhd', pattern, v)
        attn_out = jnp.einsum('bqhd,hdm->bqm', z, W_O) + b_O
        return attn_out

    def _L1_ffn_ref(x, w_gate, w_up, w_down):
        import jax, jax.numpy as jnp
        import numpy as np
        DIM = 128
        HIDDEN = 384
        SCALE = 1.0 / 127.0

        def _dequant(w_int, dtype):
            return w_int.astype(dtype) * jnp.asarray(SCALE, dtype)
        wg = _dequant(w_gate, x.dtype)
        wu = _dequant(w_up, x.dtype)
        wd = _dequant(w_down, x.dtype)
        gate = jnp.einsum('bsd,hd->bsh', x, wg)
        up = jnp.einsum('bsd,hd->bsh', x, wu)
        h = jax.nn.silu(gate) * up
        return jnp.einsum('bsh,dh->bsd', h, wd)
    x = L0_attn_x
    xn = _layernorm(x, axis=-1)
    s = _L0_attn_ref(xn, L0_attn_w_qkv, L0_attn_w_out, L0_attn_b_out, L0_attn_gamma, L0_attn_beta)
    g = _silu(_L0_ffn_ref(xn, L0_ffn_attention_mask, L0_ffn_position_ids, L0_ffn_router_w, L0_ffn_router_b, L0_ffn_wq, L0_ffn_wk, L0_ffn_wv, L0_ffn_wo, L0_ffn_w1, L0_ffn_w2, L0_ffn_ln1, L0_ffn_ln2))
    x = x + s * g
    xn = _layernorm(x, axis=-1)
    s = _L1_attn_ref(xn, L1_attn_W_Q, L1_attn_W_K, L1_attn_W_V, L1_attn_W_O, L1_attn_b_Q, L1_attn_b_K, L1_attn_b_V, L1_attn_b_O)
    g = _silu(_L1_ffn_ref(xn, L1_ffn_w_gate, L1_ffn_w_up, L1_ffn_w_down))
    x = x + s * g
    return x

_drawn_inputs = setup_inputs


def setup_inputs(seed=0):
    import zlib

    import numpy as np

    out = dict(_drawn_inputs(seed))
    spreads = {'L0_attn_b_out': (0.0, 0.1),
     'L0_attn_gamma': (1.0, 0.2),
     'L0_attn_beta': (0.0, 0.1),
     'L0_ffn_ln1': (1.0, 0.6),
     'L0_ffn_ln2': (1.0, 0.6),
     'L1_attn_b_Q': (0.0, 0.8),
     'L1_attn_b_K': (0.0, 0.8),
     'L1_attn_b_V': (0.0, 0.1),
     'L1_attn_b_O': (0.0, 0.1)}
    factors = {'L0_ffn_wq': 8.0,
     'L0_ffn_wk': 8.0,
     'L0_ffn_wv': 8.0,
     'L0_ffn_wo': 8.0,
     'L0_ffn_w1': 8.0,
     'L0_ffn_w2': 8.0,
     'L1_attn_W_Q': 8.0,
     'L1_attn_W_K': 7.97}
    for name, (base, spread) in spreads.items():
        noise = np.random.default_rng([zlib.crc32(name.encode()), seed]).standard_normal(out[name].shape)
        drawn = base * np.exp(spread * noise) if base else spread * noise
        out[name] = jnp.asarray(drawn.astype(out[name].dtype))
    for name, factor in factors.items():
        out[name] = (out[name] * factor).astype(out[name].dtype)
    return out
```

```python
from contextlib import ExitStack
import math

import numpy as np
import concourse.bass as bass
from concourse import mybir

F32 = mybir.dt.float32
F32R = mybir.dt.float32r
BF16 = mybir.dt.bfloat16
I32 = mybir.dt.int32
ALU = mybir.AluOpType
ACT = mybir.ActivationFunctionType
AX_X = mybir.AxisListType.X

P = 128
S = 2048
D = 128
T = S // P
C = 512
NC = S // C
TC = C // P
H = 16
HD0 = D // H
PARTS = 3
ROWS0 = PARTS * PARTS * HD0
GH = 4
G = H // GH
LN_EPS = 1e-5
KERN_EPS = 1e-6
RMS_EPS = 1e-6
SEL = S // 8 - 1
SLOTS = SEL + 1
NS = SLOTS // P
SELS = [P, SEL - P]
MP = 512
MT = MP // P
F0 = 512
FT = F0 // P
HD1 = 64
F1 = 384
F1T = F1 // P
Q_SCALE = 1.0 / 127.0
NEG = -1e30
EXP_MAX = 80.0


class Chain:

    def __init__(self, engine, semaphore):
        self.engine, self.semaphore, self.steps = engine, semaphore, 0

    def __call__(self, instruction):
        instruction.then_inc(self.semaphore, 1)
        self.steps += 1
        self.engine.wait_ge(self.semaphore, self.steps)


def rsqrt_refine(link, nc, out, root, square, work):
    link(nc.vector.reciprocal(out, root))
    link(nc.vector.tensor_tensor(work, out, out, ALU.mult))
    link(nc.vector.tensor_tensor(work, work, square, ALU.mult))
    link(nc.vector.tensor_scalar(work, work, -0.5, 1.5, ALU.mult, ALU.add))
    link(nc.vector.tensor_tensor(out, out, work, ALU.mult))


class Shared:
    pass


def prepare(nc, a, sh):
    with ExitStack() as ctx:
        def sb(name, shape, dt=F32):
            return ctx.enter_context(nc.sbuf_tensor(name, shape, dt))

        def sem(name):
            return ctx.enter_context(nc.semaphore(name))

        wqkv = sb("wqkv", [P, 3 * D])
        w_parts = sb("w_parts", [P, 3, D])
        stats = sb("stats", [P, T, 6])
        moments = sb("moments", [P, T, 2])
        var_eps = sb("var_eps", [P, T])
        root = sb("root", [P, T])
        rstd = sb("rstd", [P, T])
        newton = sb("newton", [P, T])
        parts = sb("parts", [P, 2, PARTS, S], BF16)
        rest = sb("rest", [P, 2, 2, C])

        x_loaded = [sem(f"x_loaded{c}") for c in range(NC)]
        w_loaded = sem("w_loaded")
        w_parted = sem("w_parted")
        ident_zero = sem("ident_zero")
        ident_done = sem("ident_done")
        var_done = sem("var_done")
        root_done = sem("root_done")
        norm_step = sem("norm_step")
        normed = sem("normed")
        turned = sem("turned")
        turned_out = sem("turned_out")
        projected = sem("projected")
        part1_done = sem("part1_done")
        rest1_done = sem("rest1_done")
        part2_done = sem("part2_done")
        part3_done = sem("part3_done")
        v_projected = sem("v_projected")
        v_out = sem("v_out")
        parts_stored = sem("parts_stored")
        cs_done = sem("cs_done")

        x_view = a["L0_attn_x"][0].rearrange("(t p) d -> p t d", p=P)
        bank = sh.bank

        block = ctx.enter_context(nc.Block())

        @block.sync
        def _(sp):
            for c in range(NC):
                sp.dma_start(sh.x[:, c * TC:(c + 1) * TC, :], x_view[:, c * TC:(c + 1) * TC, :])\
                    .then_inc(x_loaded[c], 16)
            sp.dma_start(wqkv[:, :], a["L0_attn_w_qkv"]).then_inc(w_loaded, 16)
            for m in range(2):
                for n in range(PARTS):
                    last = [part1_done, part2_done, part3_done][n]
                    sp.wait_ge(last, NC * (m + 1))
                    sp.dma_start(sh.parts_dram[m, n], parts[:, m, n, :]).then_inc(parts_stored, 16)
            sp.wait_ge(parts_stored, 16 * 2 * PARTS)

        @block.gpsimd
        def _(pool):
            nc.gpsimd.memset(sh.ident[:, :], 0.0).then_inc(ident_zero, 1)
            nc.gpsimd.memset(sh.ones[:, :], 1.0).then_inc(cs_done, 1)
            pool.wait_ge(ident_zero, 1)
            nc.gpsimd.affine_select(out=sh.ident[:, :], in_=sh.ident[:, :], compare_op=ALU.not_equal, fill=1.0,
                                    base=0, pattern=[[-1, P]], channel_multiplier=1).then_inc(ident_done, 1)
            pool.wait_ge(w_loaded, 16)
            for m in range(3):
                nc.gpsimd.tensor_copy(w_parts[:, m, :].rearrange("d (h j) -> d h j", j=HD0),
                                      wqkv[:, :].rearrange("d (h c j) -> d c h j", c=3, j=HD0)[:, m])\
                    .then_inc(w_parted, 1)

        @block.vector
        def _(dve):
            link = Chain(dve, norm_step)
            for t in range(T):
                if t % TC == 0:
                    dve.wait_ge(x_loaded[t // TC], 16)
                stat = nc.vector.bn_stats(stats[:, t, :], sh.x[:, t, :])
            link(stat)
            for t in range(T):
                last = nc.vector.bn_aggr(moments[:, t, :], stats[:, t, :])
            link(last)
            nc.vector.tensor_scalar(var_eps[:, :], moments[:, :, 1], LN_EPS, None, ALU.add).then_inc(var_done, 1)
            dve.wait_ge(root_done, 1)
            rsqrt_refine(link, nc, rstd[:, :], root[:, :], var_eps[:, :], newton[:, :])
            for t in range(T):
                nc.vector.tensor_scalar(sh.xa[:, t, 0:D], sh.x[:, t, :], moments[:, t, 0:1], rstd[:, t:t + 1],
                                        ALU.subtract, ALU.mult).then_inc(normed, 1)
            for n in range(2 * NC):
                m, c = n // NC, n % NC
                at = slice(c * C, (c + 1) * C)
                dve.wait_ge(part1_done, n + 1)
                if n >= 2:
                    dve.wait_ge(part3_done, n - 1)
                nc.vector.tensor_tensor(rest[:, n % 2, 0, :], bank[4 + n % 2], parts[:, m, 0, at],
                                        ALU.subtract).then_inc(rest1_done, 1)
                dve.wait_ge(part2_done, n + 1)
                nc.vector.tensor_tensor(parts[:, m, 2, at], rest[:, n % 2, 0, :], parts[:, m, 1, at],
                                        ALU.subtract).then_inc(part3_done, 1)
            for c in range(NC):
                dve.wait_ge(v_projected, c + 1)
                nc.vector.tensor_copy(sh.v0[:, c * TC:(c + 1) * TC, :],
                                      bank[6 + c % 2].rearrange("p (t d) -> p t d", d=D)).then_inc(v_out, 1)

        @block.scalar
        def _(act):
            act.wait_ge(var_done, 1)
            nc.scalar.activation(root[:, :], var_eps[:, :], ACT.Sqrt).then_inc(root_done, 1)
            for c in range(NC):
                act.wait_ge(turned, c + 1)
                nc.scalar.copy(sh.xnT[:, c * C:(c + 1) * C], bank[c]).then_inc(turned_out, 1)
            for n in range(2 * NC):
                m, c = n // NC, n % NC
                at = slice(c * C, (c + 1) * C)
                act.wait_ge(projected, n + 1)
                nc.scalar.copy(parts[:, m, 0, at], bank[4 + n % 2]).then_inc(part1_done, 1)
                act.wait_ge(rest1_done, n + 1)
                nc.scalar.copy(parts[:, m, 1, at], rest[:, n % 2, 0, :]).then_inc(part2_done, 1)

        @block.tensor
        def _(pe):
            pe.wait_ge(ident_done, 1)
            for t in range(T):
                pe.wait_ge(normed, t + 1)
                last = nc.tensor.transpose(bank[t // TC][:, (t % TC) * P:(t % TC + 1) * P], sh.xa[:, t, 0:D],
                                           sh.ident[:, :])
                if t % TC == TC - 1:
                    last.then_inc(turned, 1)
            pe.wait_ge(w_parted, 3)
            for n in range(2 * NC):
                m, c = n // NC, n % NC
                pe.wait_ge(turned_out, c + 1)
                if n >= 2:
                    pe.wait_ge(rest1_done, n - 1)
                nc.tensor.matmul(bank[4 + n % 2], w_parts[:, m, :], sh.xnT[:, c * C:(c + 1) * C],
                                 start=True, stop=True).then_inc(projected, 1)
            for c in range(NC):
                if c >= 2:
                    pe.wait_ge(v_out, c - 1)
                for j in range(TC):
                    t = c * TC + j
                    last = nc.tensor.matmul(bank[6 + c % 2][:, j * P:(j + 1) * P], sh.xnT[:, t * P:(t + 1) * P],
                                            w_parts[:, 2, :], start=True, stop=True)
                last.then_inc(v_projected, 1)


def attention0(nc, a, sh):
    with ExitStack() as ctx:
        def sb(name, shape, dt=F32):
            return ctx.enter_context(nc.sbuf_tensor(name, shape, dt))

        def sem(name):
            return ctx.enter_context(nc.semaphore(name))

        VW = 32
        WR = 4
        NB = 2
        LOADS = 2 * PARTS * PARTS
        ACT_HEADS = (0, 1)
        DVE_HEADS = (2, 3)
        q_rows = [sb(f"q_rows{n}", [P, GH, S], BF16) for n in range(NB)]
        k_rows = [sb(f"k_rows{n}", [P, GH, S], BF16) for n in range(NB)]
        v_cols = [sb(f"v_cols{n}", [P, T, GH, VW]) for n in range(NB)]
        w = sb("w0", [P, WR, GH, C])
        o_sb = sb("o_sb", [P, C])
        den = sb("den", [P, TC, GH])

        rows_loaded = [sem(f"rows_loaded{n}") for n in range(NB)]
        v_set = sem("v_set")
        v_copied = sem("v_copied")
        scored = sem("scored")
        act_relu = sem("act_relu")
        dve_relu = sem("dve_relu")
        weighted = sem("weighted")
        out_copied = sem("out_copied")
        out_turned = sem("out_turned")
        den_step = sem("den_step")
        out_done = sem("out_done")

        bank = sh.bank
        score_bank = bank[0:GH]
        out_bank = bank[4]
        turn_bank = bank[5]
        turn_view = turn_bank.rearrange("p (t h v) -> p t h v", t=TC, h=GH)

        block = ctx.enter_context(nc.Block())


        @block.sync
        def _(sp):
            for group in range(G):
                par = group % NB
                if group >= NB:
                    sp.wait_ge(weighted, WR + (group - NB + 1) * NC * T)
                heads = slice(group * GH * HD0, (group + 1) * GH * HD0)
                for n in range(PARTS):
                    for r in range(PARTS):
                        row = (n * PARTS + r) * HD0
                        sp.dma_start(q_rows[par][row:row + HD0, :, :],
                                     sh.parts_dram[0, n, heads, :].rearrange("(h j) s -> j h s", j=HD0))\
                            .then_inc(rows_loaded[par], 16)
                        sp.dma_start(k_rows[par][row:row + HD0, :, :],
                                     sh.parts_dram[1, r, heads, :].rearrange("(h j) s -> j h s", j=HD0))\
                            .then_inc(rows_loaded[par], 16)

        @block.gpsimd
        def _(pool):
            pool.sem_inc(weighted, WR)
            pool.sem_inc(act_relu, len(ACT_HEADS))
            pool.sem_inc(dve_relu, len(DVE_HEADS))
            pool.sem_inc(out_copied, 1)
            pool.sem_inc(out_done, 1)
            for n in range(NB):
                nc.gpsimd.memset(v_cols[n][:, :, :, HD0 + 1:VW], 0.0)
                nc.gpsimd.memset(v_cols[n][:, :, :, HD0:HD0 + 1], 1.0)
            for group in range(G):
                if group >= NB:
                    pool.wait_ge(weighted, WR + (group - NB + 1) * NC * T)
                heads = sh.v0[:, :, group * GH * HD0:(group + 1) * GH * HD0]
                nc.gpsimd.tensor_copy(v_cols[group % NB][:, :, :, 0:HD0],
                                      heads.rearrange("p t (h j) -> p t h j", j=HD0)).then_inc(v_copied, 1)

        @block.tensor
        def _(pe):
            def scores(par, done, kt, qc):
                for h in range(GH):
                    if h in ACT_HEADS:
                        pe.wait_ge(act_relu, (done + kt) * len(ACT_HEADS) + ACT_HEADS.index(h) + 1)
                    else:
                        pe.wait_ge(dve_relu, (done + kt) * len(DVE_HEADS) + DVE_HEADS.index(h) + 1)
                    nc.tensor.matmul(score_bank[h], k_rows[par][0:ROWS0, h, kt * P:(kt + 1) * P],
                                     q_rows[par][0:ROWS0, h, bass.ds(qc * C, C)],
                                     start=True, stop=True).then_inc(scored, 1)

            def weigh(par, done, kt):
                pe.wait_ge(act_relu, (done + kt + 2) * len(ACT_HEADS))
                pe.wait_ge(dve_relu, (done + kt + 2) * len(DVE_HEADS))
                for h in range(GH):
                    last = nc.tensor.matmul(out_bank[h * VW:(h + 1) * VW, :], v_cols[par][:, kt, h, :],
                                            w[:, kt % WR, h, :], start=(kt == 0), stop=(kt == T - 1))
                last.then_inc(weighted, 1)

            with pe.Fori(0, G // NB) as pair:
                for par in range(NB):
                    with pe.Fori(0, NC) as qc:
                        pe.wait_ge(rows_loaded[par], (pair + 1) * (16 * LOADS))
                        pe.wait_ge(v_copied, pair * NB + (par + 1))
                        turn = pe.snap(pair * (NB * NC) + (par * NC) + qc)
                        done = pe.snap(turn * T)
                        scores(par, done, 0, qc)
                        for kt in range(1, T):
                            scores(par, done, kt, qc)
                            if kt == 1:
                                pe.wait_ge(out_copied, turn + 1)
                            weigh(par, done, kt - 1)
                        weigh(par, done, T - 1)
                        pe.wait_ge(out_copied, turn + 2)
                        pe.wait_ge(out_done, turn + 1)
                        for j in range(TC):
                            last = nc.tensor.transpose(turn_bank[:, j * P:(j + 1) * P], o_sb[:, j * P:(j + 1) * P],
                                                       sh.ident[:, :])
                        last.then_inc(out_turned, 1)

        @block.scalar
        def _(act):
            with act.Fori(0, G * NC) as turn:
                for kt in range(T):
                    act.wait_ge(weighted, turn * T + (kt + 1))
                    for h in ACT_HEADS:
                        act.wait_ge(scored, turn * (T * GH) + (kt * GH + h + 1))
                        nc.scalar.activation(w[:, kt % WR, h, :], score_bank[h], ACT.Relu).then_inc(act_relu, 1)

        @block.vector
        def _(dve):
            with dve.Fori(0, G) as group:
                with dve.Fori(0, NC) as qc:
                    turn = dve.snap(group * NC + qc)
                    for kt in range(T):
                        dve.wait_ge(weighted, turn * T + (kt + 1))
                        for h in DVE_HEADS:
                            dve.wait_ge(scored, turn * (T * GH) + (kt * GH + h + 1))
                            nc.vector.tensor_scalar(w[:, kt % WR, h, :], score_bank[h], 0.0, None, ALU.max)\
                                .then_inc(dve_relu, 1)
                    dve.wait_ge(weighted, turn * T + (WR + T))
                    nc.vector.tensor_copy(o_sb[:, :], out_bank).then_inc(out_copied, 1)
                    dve.wait_ge(out_turned, turn + 1)
                    nc.vector.tensor_scalar(den[:, :, :], turn_view[:, :, :, HD0], KERN_EPS * math.sqrt(HD0), None,
                                            ALU.add).then_inc(den_step, 1)
                    dve.wait_ge(den_step, turn * 2 + 1)
                    nc.vector.reciprocal(den[:, :, :], den[:, :, :]).then_inc(den_step, 1)
                    dve.wait_ge(den_step, turn * 2 + 2)
                    nc.vector.tensor_tensor(sh.o0[:, bass.ds(qc * TC, TC), bass.ds(group * GH, GH), :],
                                            turn_view[:, :, :, 0:HD0],
                                            den[:, :, :].unsqueeze(3).to_broadcast([P, TC, GH, HD0]),
                                            ALU.mult).then_inc(out_done, 1)


def routed0(nc, a, sh):
    with ExitStack() as ctx:
        def sb(name, shape, dt=F32):
            return ctx.enter_context(nc.sbuf_tensor(name, shape, dt))

        def sem(name):
            return ctx.enter_context(nc.semaphore(name))

        TWO_PI = (6.28125, 0.0019350051879882812, 3.019916050561733e-07)
        ROUND = 1.5 * 2.0 ** 23
        HALF = HD0 // 2
        INV_FREQ = [float(f) for f in np.float32(1.0) / np.float32(10000.0) ** (
            np.arange(0, HD0, 2, dtype=np.float32) / np.float32(HD0))]
        GELU_C = 2.0 * math.sqrt(2.0 / math.pi)

        router_b = sb("router_b", [P, D])
        bias_b = sb("bias_b", [P, 1])
        pos_own = sb("pos_own", [P, MT], I32)
        pos_last = sb("pos_last", [P, 1], I32)
        mask = sb("mask", [P, MT, MP])
        w_att = sb("w_att", [P, 4, D])
        w1 = sb("w1", [P, F0])
        w2 = sb("w2", [P, FT, D])
        ln_b = sb("ln_b", [P, 2, D])
        iota = sb("iota", [P, SLOTS])
        lower = sb("lower", [P, P])
        head_rows = sb("head_rows", [P, H])
        freq = sb("freq", [P, HALF])
        work = sb("work", [P, S])
        diag = sb("diag", [P, T, P])
        counts = sb("counts", [P, 3, T])
        rank = sb("rank", [P, T])
        thr_part = sb("thr_part", [P, 1])
        keep = sb("keep", [P, T])
        onehot = sb("onehot", [P, T, SLOTS])
        onehotT = sb("onehotT", [P, NS, S])
        row_last = sb("row_last", [P, SLOTS])
        mask_cols = sb("mask_cols", [P, MT, SLOTS])
        mask_sel = sb("mask_sel", [P, NS, SLOTS])
        xs = sb("xs", [P, NS, D + 2])
        angle = sb("angle", [P, NS, HALF])
        turns = sb("turns", [P, NS, HALF])
        trig = sb("trig", [P, NS, 2, HALF])
        square = sb("square", [P, 2, NS])
        root = sb("root_sel", [P, 2, NS])
        rms = sb("rms", [P, 2, NS])
        newton = sb("newton_sel", [P, 2, NS])
        hn = sb("hn", [P, NS, D])
        hnT = sb("hnT", [P, SLOTS])
        rope = sb("rope", [P, 2, 2 * H, HALF])
        qk = sb("qk", [P, NS, 2 * H, 2, HALF])
        vs = sb("vs", [P, NS, D])
        kT = sb("kT", [P, SLOTS])
        qT = sb("qT", [P, H, SLOTS])
        prob = sb("prob", [P, H, NS, SEL])
        probT = sb("probT", [P, 4, NS, SLOTS])
        top = sb("top", [P, H, NS])
        total = sb("total", [P, NS, H])
        o = sb("o_sel", [P, NS, D])
        oT = sb("oT", [P, SLOTS])
        x1 = sb("x1_sel", [P, NS, D])
        gate = sb("gate_sel", [P, 3, FT * SLOTS])
        proc = sb("proc", [P, NS, D])
        sig = work[:, :].rearrange("p (t d) -> p t d", d=D)

        router_loaded = sem("router_loaded")
        mask_loaded = sem("mask_loaded")
        att_loaded = sem("att_loaded")
        mlp_loaded = sem("mlp_loaded")
        pool_step = sem("pool_step")
        consts_set = sem("consts_set")
        diag_done = sem("diag_done")
        spread = sem("spread")
        ranked = sem("ranked")
        thr_ready = sem("thr_ready")
        thr_spread = sem("thr_spread")
        gathered = sem("gathered")
        tail_summed = sem("tail_summed")
        clamped = sem("clamped")
        placed = sem("placed")
        placed_out = sem("placed_out")
        cols_taken = sem("cols_taken")
        cols_out = sem("cols_out")
        mask_taken = sem("mask_taken")
        angle_ready = sem("angle_ready")
        trig_done = sem("trig_done")
        square_ready = sem("square_ready")
        root_done = sem("root_sel_done")
        hn_done = sem("hn_done")
        hn_turned = sem("hn_turned")
        hnT_done = sem("hnT_done")
        qkv_done = sem("qkv_done")
        roped = sem("roped")
        qk_turned = sem("qk_turned")
        qkT_done = sem("qkT_done")
        scored = sem("scored_sel")
        masked = sem("masked_sel")
        exped = sem("exped_sel")
        prob_turned = sem("prob_turned")
        probT_done = sem("probT_done")
        weighted = sem("weighted_sel")
        o_done = sem("o_sel_done")
        o_turned = sem("o_turned")
        oT_done = sem("oT_done")
        mixed = sem("mixed")
        hidden = sem("hidden")
        squared = sem("squared")
        inner_done = sem("inner_done")
        gate_exp = sem("gate_exp")
        gated = sem("gated")
        downed = sem("downed")
        proc_done = sem("proc_done")
        scattered = sem("scattered")
        combined = sem("combined")
        sig_exp = sem("sig_exp")
        step = sem("routed_step")

        bank = sh.bank
        weight = sh.xa[:, :, D]
        mask_dram = a["L0_ffn_attention_mask"][0, 0]
        pos_dram = a["L0_ffn_position_ids"][0]

        block = ctx.enter_context(nc.Block())

        @block.sync
        def _(sp):
            sp.dma_start(router_b[:, :], a["L0_ffn_router_w"].rearrange("d o -> (o d)").partition_broadcast(P))\
                .then_inc(router_loaded, 16)
            sp.dma_start(bias_b[:, :], a["L0_ffn_router_b"].partition_broadcast(P)).then_inc(router_loaded, 16)
            sp.dma_start(pos_own[:, :], pos_dram.rearrange("(t p) -> p t", p=P),
                         allow_slow_non_contiguous=True).then_inc(router_loaded, 16)
            sp.dma_start(pos_last[:, :], pos_dram[MP - 1:MP].partition_broadcast(P)).then_inc(router_loaded, 16)
            sp.dma_start(mask[:, :, :], mask_dram.rearrange("(t p) c -> p t c", p=P)).then_inc(mask_loaded, 16)
            for n, name in enumerate(("wq", "wk", "wv", "wo")):
                sp.dma_start(w_att[:, n, :], a["L0_ffn_" + name]).then_inc(att_loaded, 16)
            sp.dma_start(ln_b[:, 0, :], a["L0_ffn_ln1"].partition_broadcast(P)).then_inc(att_loaded, 16)
            sp.dma_start(ln_b[:, 1, :], a["L0_ffn_ln2"].partition_broadcast(P)).then_inc(att_loaded, 16)
            sp.dma_start(w1[:, :], a["L0_ffn_w1"]).then_inc(mlp_loaded, 16)
            sp.dma_start(w2[:, :, :], a["L0_ffn_w2"].rearrange("(t p) d -> p t d", p=P)).then_inc(mlp_loaded, 16)

        @block.gpsimd
        def _(pool):
            link = Chain(pool, pool_step)
            nc.gpsimd.iota(iota[:, :], pattern=[[1, SLOTS]], base=0, channel_multiplier=0,
                           allow_small_or_imprecise_dtypes=True)
            for n in range(HALF):
                nc.gpsimd.memset(freq[:, n:n + 1], INV_FREQ[n])
            link(nc.gpsimd.memset(lower[:, :], 1.0))
            link(nc.gpsimd.affine_select(out=lower[:, :], in_=lower[:, :], compare_op=ALU.is_gt, fill=0.0,
                                         base=0, pattern=[[-1, P]], channel_multiplier=1))
            link(nc.gpsimd.memset(head_rows[:, :], 1.0 / math.sqrt(HD0)))
            link(nc.gpsimd.affine_select(out=head_rows[:, :], in_=head_rows[:, :], compare_op=ALU.is_ge, fill=0.0,
                                         base=0, pattern=[[-HD0, H]], channel_multiplier=1))
            nc.gpsimd.affine_select(out=head_rows[:, :], in_=head_rows[:, :], compare_op=ALU.is_ge, fill=0.0,
                                    base=HD0 - 1, pattern=[[HD0, H]], channel_multiplier=-1)\
                .then_inc(consts_set, 1)

        @block.vector
        def _(dve):
            link = Chain(dve, step)
            dve.wait_ge(router_loaded, 64)
            for t in range(T):
                last = nc.vector.tensor_tensor_reduce(out=diag[:, t, :], in0=sh.xa[:, t, 0:D], in1=router_b[:, :],
                                                      scale=1.0, scalar=0.0, op0=ALU.mult, op1=ALU.add,
                                                      accum_out=rank[:, t:t + 1])
            link(last)
            link(nc.vector.tensor_scalar(weight, rank[:, :], bias_b[:, 0:1], None, ALU.add))
            nc.vector.tensor_copy(sh.xa[:, 0:MT, D + 1], pos_own[:, :])
            link(nc.vector.tensor_copy(sh.xa[:, MT:T, D + 1], pos_last[:, 0:1].to_broadcast([P, T - MT])))
            for t in range(T):
                nc.vector.tensor_scalar(diag[:, t, :], sh.ident[:, :], sh.xa[:, t, D:D + 1], None, ALU.mult)\
                    .then_inc(diag_done, 1)
            link(nc.vector.memset(counts[:, 0, 0:1], 0.0))
            dve.wait_ge(spread, 1)
            dve.wait_ge(consts_set, 1)
            every = sh.psum[:, 0:NC, :].rearrange("p b c -> p (b c)")
            for t in range(T):
                own = sh.xa[:, t, D:D + 1]
                if t:
                    nc.vector.tensor_scalar(work[:, 0:t * P], every[:, 0:t * P], own, None, ALU.is_ge, ALU.add,
                                            accum_out=counts[:, 0, t:t + 1])
                nc.vector.tensor_scalar(work[:, t * P:S], every[:, t * P:S], own, None, ALU.is_gt, ALU.add,
                                        accum_out=counts[:, 1, t:t + 1])
                link(nc.vector.scalar_tensor_tensor(out=diag[:, t, :], in0=every[:, t * P:(t + 1) * P], scalar=own,
                                                    in1=lower[:, :], op0=ALU.is_equal, op1=ALU.mult,
                                                    accum_out=counts[:, 2, t:t + 1]))
            link(nc.vector.tensor_tensor(rank[:, :], counts[:, 0, :], counts[:, 1, :], ALU.add))
            link(nc.vector.tensor_tensor(rank[:, :], rank[:, :], counts[:, 2, :], ALU.add))
            for t in range(T):
                nc.vector.tensor_scalar(onehot[:, t, :], iota[:, :], rank[:, t:t + 1], None, ALU.is_equal)\
                    .then_inc(ranked, 1)
            nc.vector.scalar_tensor_tensor(out=keep[:, :], in0=rank[:, :], scalar=float(SEL), in1=weight,
                                           op0=ALU.is_equal, op1=ALU.mult, accum_out=thr_part[:, :])\
                .then_inc(thr_ready, 1)
            dve.wait_ge(thr_spread, 1)
            link(nc.vector.tensor_scalar(keep[:, :], weight, bank[7][:, 0:1], None, ALU.is_le))
            dve.wait_ge(tail_summed, 1)
            nc.vector.scalar_tensor_tensor(out=row_last[:, :], in0=bank[6][:, 0:SLOTS], scalar=sh.ident[:, P - 1:P],
                                           in1=onehot[:, MT - 1, :], op0=ALU.mult, op1=ALU.add)\
                .then_inc(clamped, 1)
            dve.wait_ge(gathered, 1)
            link(nc.vector.tensor_copy(xs[:, :, :], sh.psum[:, 4:4 + NS, 0:D + 2]))
            for s in range(NS):
                last = nc.vector.tensor_scalar(angle[:, s, :], freq[:, :], xs[:, s, D + 1:D + 2], None, ALU.mult)
            link(last)
            link(nc.vector.tensor_scalar(turns[:, :, :], angle[:, :, :], 1.0 / (2.0 * math.pi), ROUND,
                                         ALU.mult, ALU.add))
            link(nc.vector.tensor_scalar(turns[:, :, :], turns[:, :, :], ROUND, None, ALU.subtract))
            for part in TWO_PI:
                link(nc.vector.scalar_tensor_tensor(out=angle[:, :, :], in0=turns[:, :, :], scalar=-part,
                                                    in1=angle[:, :, :], op0=ALU.mult, op1=ALU.add))
            link(nc.vector.tensor_scalar(trig[:, :, 0, :], angle[:, :, :], math.pi / 2, None, ALU.add))
            link(nc.vector.tensor_scalar(turns[:, :, :], trig[:, :, 0, :], 3.1415925, None, ALU.is_gt))
            link(nc.vector.scalar_tensor_tensor(out=trig[:, :, 1, :], in0=turns[:, :, :], scalar=-2.0 * math.pi,
                                                in1=trig[:, :, 0, :], op0=ALU.mult, op1=ALU.add))
            link(nc.vector.tensor_copy(trig[:, :, 0, :], angle[:, :, :]))
            nc.vector.tensor_scalar(trig[:, :, :, :], trig[:, :, :, :], 3.1415925, -3.1415925, ALU.min, ALU.max)\
                .then_inc(angle_ready, 1)

            def rms_norm(n, src, turn_bank):
                for s in range(NS):
                    last = nc.vector.tensor_tensor_reduce(out=hn[:, s, :], in0=src[:, s, 0:D], in1=src[:, s, 0:D],
                                                          scale=1.0, scalar=0.0, op0=ALU.mult, op1=ALU.add,
                                                          accum_out=square[:, n, s:s + 1])
                link(last)
                nc.vector.tensor_scalar(square[:, n, :], square[:, n, :], 1.0 / D, RMS_EPS, ALU.mult, ALU.add)\
                    .then_inc(square_ready, 1)
                dve.wait_ge(root_done, n + 1)
                rsqrt_refine(link, nc, rms[:, n, :], root[:, n, :], square[:, n, :], newton[:, n, :])
                for s in range(NS):
                    nc.vector.scalar_tensor_tensor(out=hn[:, s, :], in0=src[:, s, 0:D], scalar=rms[:, n, s:s + 1],
                                                   in1=ln_b[:, n, :], op0=ALU.mult, op1=ALU.mult)\
                        .then_inc(hn_done, 1)
                dve.wait_ge(hn_turned, n + 1)
                nc.vector.tensor_copy(hnT[:, :], turn_bank[:, 0:SLOTS]).then_inc(hnT_done, 1)

            dve.wait_ge(att_loaded, 96)
            rms_norm(0, xs, bank[6])
            dve.wait_ge(trig_done, 1)
            for s in range(NS):
                dve.wait_ge(qkv_done, s + 1)
                both = bank[4 + s][:, 0:2 * D].rearrange("p (h two j) -> p h two j", two=2, j=HALF)
                sine = trig[:, s, 0:1, :].to_broadcast([P, 2 * H, HALF])
                cosine = trig[:, s, 1:2, :].to_broadcast([P, 2 * H, HALF])
                for half, op in ((0, ALU.subtract), (1, ALU.add)):
                    nc.vector.tensor_tensor(rope[:, 0, :, :], both[:, :, half, :], cosine, ALU.mult)
                    link(nc.vector.tensor_tensor(rope[:, 1, :, :], both[:, :, 1 - half, :], sine, ALU.mult))
                    link(nc.vector.tensor_tensor(qk[:, s, :, half, :], rope[:, 0, :, :], rope[:, 1, :, :], op))
                nc.vector.tensor_copy(vs[:, s, :], bank[4 + s][:, 2 * D:3 * D]).then_inc(roped, 1)
            dve.wait_ge(qk_turned, 1)
            nc.vector.tensor_copy(kT[:, :], bank[6][:, SLOTS:2 * SLOTS])
            for h in range(H):
                nc.vector.tensor_scalar(qT[:, h, :], bank[6][:, 0:SLOTS], head_rows[:, h:h + 1], None, ALU.mult)\
                    .then_inc(qkT_done, 1)
            dve.wait_ge(mask_taken, 1)
            link(nc.vector.tensor_copy(mask_sel[:, :, :], bank[7].rearrange("p (s k) -> p s k", s=NS)))

            def mask_scores(h):
                dve.wait_ge(scored, h + 1)
                for s in range(NS):
                    last = nc.vector.tensor_tensor_reduce(
                        out=prob[:, h, s, :], in0=bank[h % 2][:, s * SLOTS:s * SLOTS + SEL],
                        in1=mask_sel[:, s, 0:SEL], scale=1.0, scalar=-3.0e38, op0=ALU.add, op1=ALU.max,
                        accum_out=top[:, h, s:s + 1])
                link(last)
                nc.vector.tensor_scalar(top[:, h, :], top[:, h, :], -1.0, None, ALU.mult).then_inc(masked, 1)

            def take_probs(h):
                dve.wait_ge(prob_turned, h + 1)
                if h >= 4:
                    dve.wait_ge(weighted, h - 3)
                nc.vector.tensor_copy(probT[:, h % 4, :, :], bank[2 + h % 2].rearrange("p (k q) -> p k q", k=NS))\
                    .then_inc(probT_done, 1)

            for h in range(H + 2):
                if h < H:
                    mask_scores(h)
                if h >= 2:
                    take_probs(h - 2)
            link(nc.vector.reciprocal(total[:, :, :], total[:, :, :]))
            dve.wait_ge(weighted, H)
            nc.vector.tensor_tensor(o[:, :, :].rearrange("p s (h j) -> p s h j", j=HD0),
                                    bank[4][:, 0:NS * D].rearrange("p (s h j) -> p s h j", s=NS, j=HD0),
                                    total[:, :, :].unsqueeze(3).to_broadcast([P, NS, H, HD0]), ALU.mult)\
                .then_inc(o_done, 1)
            dve.wait_ge(o_turned, 1)
            nc.vector.tensor_copy(oT[:, :], bank[5][:, 0:SLOTS]).then_inc(oT_done, 1)
            dve.wait_ge(mixed, 1)
            link(nc.vector.tensor_tensor(x1[:, :, :], bank[6][:, 0:NS * D].rearrange("p (s d) -> p s d", s=NS),
                                         xs[:, :, 0:D], ALU.add))
            rms_norm(1, x1, bank[7])
            inner = sh.psum[:, 0:2, :].rearrange("p b c -> p (b c)")
            dve.wait_ge(squared, 1)
            link(nc.vector.tensor_scalar(gate[:, 0, :], gate[:, 0, :], 0.044715, 1.0, ALU.mult, ALU.add))
            link(nc.vector.tensor_tensor(gate[:, 0, :], gate[:, 0, :], inner, ALU.mult))
            nc.vector.tensor_scalar(gate[:, 0, :], gate[:, 0, :], -EXP_MAX / GELU_C, None, ALU.max)\
                .then_inc(inner_done, 1)
            dve.wait_ge(gate_exp, 1)
            link(nc.vector.tensor_scalar(gate[:, 1, :], gate[:, 1, :], 1.0, None, ALU.add))
            link(nc.vector.reciprocal(gate[:, 1, :], gate[:, 1, :]))
            nc.vector.tensor_tensor(gate[:, 2, :], gate[:, 1, :], inner, ALU.mult).then_inc(gated, 1)
            dve.wait_ge(downed, 1)
            link(nc.vector.tensor_tensor(proc[:, :, :], bank[4][:, 0:NS * D].rearrange("p (s d) -> p s d", s=NS),
                                         x1[:, :, :], ALU.add))
            for s in range(NS):
                nc.vector.tensor_scalar(proc[:, s, :], proc[:, s, :], xs[:, s, D:D + 1], None, ALU.mult)\
                    .then_inc(proc_done, 1)
            for c in range(NC):
                dve.wait_ge(scattered, c + 1)
                for j in range(TC):
                    t = c * TC + j
                    last = nc.vector.scalar_tensor_tensor(out=sh.g[:, t, :], in0=sh.xa[:, t, 0:D],
                                                          scalar=keep[:, t:t + 1], in1=bank[c][:, j * P:(j + 1) * P],
                                                          op0=ALU.mult, op1=ALU.add)
                link(last)
                nc.vector.tensor_scalar(sig[:, c * TC:(c + 1) * TC, :], sh.g[:, c * TC:(c + 1) * TC, :], -EXP_MAX,
                                        None, ALU.max).then_inc(combined, 1)
            for c in range(NC):
                at = slice(c * TC, (c + 1) * TC)
                dve.wait_ge(sig_exp, c + 1)
                link(nc.vector.tensor_scalar(sig[:, at, :], sig[:, at, :], 1.0, None, ALU.add))
                link(nc.vector.reciprocal(sig[:, at, :], sig[:, at, :]))
                link(nc.vector.tensor_tensor(sh.g[:, at, :], sh.g[:, at, :], sig[:, at, :], ALU.mult))

        @block.scalar
        def _(act):
            for n in range(NS * NC):
                s, c = n // NC, n % NC
                act.wait_ge(placed, n + 1)
                nc.scalar.copy(onehotT[:, s, c * C:(c + 1) * C], bank[c]).then_inc(placed_out, 1)
            for n in range(2):
                act.wait_ge(cols_taken, n + 1)
                nc.scalar.copy(mask_cols[:, 2 * n:2 * n + 2, :], bank[n].rearrange("p (c s) -> p c s", c=2))\
                    .then_inc(cols_out, 1)
            act.wait_ge(square_ready, 1)
            nc.scalar.activation(root[:, 0, :], square[:, 0, :], ACT.Sqrt).then_inc(root_done, 1)
            act.wait_ge(angle_ready, 1)
            nc.scalar.activation(trig[:, :, :, :], trig[:, :, :, :], ACT.Sin).then_inc(trig_done, 1)
            for h in range(H):
                act.wait_ge(masked, h + 1)
                for s in range(NS):
                    last = nc.scalar.activation(prob[:, h, s, :], prob[:, h, s, :], ACT.Exp, bias=top[:, h, s:s + 1],
                                                accum_out=total[:, s, h:h + 1])
                last.then_inc(exped, 1)
            act.wait_ge(square_ready, 2)
            nc.scalar.activation(root[:, 1, :], square[:, 1, :], ACT.Sqrt).then_inc(root_done, 1)
            act.wait_ge(hidden, 1)
            nc.scalar.activation(gate[:, 0, :], sh.psum[:, 0:2, :].rearrange("p b c -> p (b c)"), ACT.Square)\
                .then_inc(squared, 1)
            act.wait_ge(inner_done, 1)
            nc.scalar.activation(gate[:, 1, :], gate[:, 0, :], ACT.Exp, scale=-GELU_C).then_inc(gate_exp, 1)
            for c in range(NC):
                act.wait_ge(combined, c + 1)
                nc.scalar.activation(sig[:, c * TC:(c + 1) * TC, :], sig[:, c * TC:(c + 1) * TC, :], ACT.Exp,
                                     scale=-1.0).then_inc(sig_exp, 1)

        @block.tensor
        def _(pe):
            for t in range(T):
                pe.wait_ge(diag_done, t + 1)
                last = nc.tensor.matmul(bank[t // TC][:, (t % TC) * P:(t % TC + 1) * P], sh.ones[:, :], diag[:, t, :],
                                        start=True, stop=True)
            last.then_inc(spread, 1)
            pe.wait_ge(ranked, T)
            for s in range(NS):
                for t in range(T):
                    last = nc.tensor.matmul(bank[4 + s][:, 0:D + 2], onehot[:, t, s * P:(s + 1) * P], sh.xa[:, t, :],
                                            start=(t == 0), stop=(t == T - 1))
            last.then_inc(gathered, 1)
            for t in range(MT, T):
                last = nc.tensor.matmul(bank[6][:, 0:SLOTS], sh.ones[:, :], onehot[:, t, :],
                                        start=(t == MT), stop=(t == T - 1))
            last.then_inc(tail_summed, 1)
            pe.wait_ge(thr_ready, 1)
            nc.tensor.matmul(bank[7][:, 0:1], sh.ones[:, :], thr_part[:, :], start=True, stop=True)\
                .then_inc(thr_spread, 1)
            for n in range(NS * NC):
                s, c = n // NC, n % NC
                if n >= NC:
                    pe.wait_ge(placed_out, n - NC + 1)
                for j in range(TC):
                    t = c * TC + j
                    last = nc.tensor.transpose(bank[c][:, j * P:(j + 1) * P], onehot[:, t, s * P:(s + 1) * P],
                                               sh.ident[:, :])
                last.then_inc(placed, 1)
            pe.wait_ge(mask_loaded, 16)
            pe.wait_ge(clamped, 1)
            pe.wait_ge(placed_out, NS * NC)

            def rows(r):
                return row_last[:, :] if r == MT - 1 else onehot[:, r, :]

            for c in range(MT):
                for r in range(MT):
                    last = nc.tensor.matmul(bank[c // 2][:, (c % 2) * SLOTS:(c % 2 + 1) * SLOTS],
                                            mask[:, r, c * P:(c + 1) * P], rows(r),
                                            start=(r == 0), stop=(r == MT - 1))
                if c % 2:
                    last.then_inc(cols_taken, 1)
            pe.wait_ge(cols_out, 2)
            pe.wait_ge(clamped, 1)
            for s in range(NS):
                for c in range(MT):
                    last = nc.tensor.matmul(bank[7][:, s * SLOTS:(s + 1) * SLOTS], mask_cols[:, c, s * P:(s + 1) * P],
                                            rows(c), start=(c == 0), stop=(c == MT - 1))
            last.then_inc(mask_taken, 1)

            def turn_hn(n, turn_bank):
                for s in range(NS):
                    pe.wait_ge(hn_done, n * NS + s + 1)
                    last = nc.tensor.transpose(turn_bank[:, s * P:(s + 1) * P], hn[:, s, :], sh.ident[:, :])
                last.then_inc(hn_turned, 1)
                pe.wait_ge(hnT_done, n + 1)

            turn_hn(0, bank[6])
            for s in range(NS):
                nc.tensor.matmul(bank[4 + s][:, 0:3 * D], hnT[:, s * P:(s + 1) * P],
                                 w_att[:, 0:3, :], start=True, stop=True).then_inc(qkv_done, 1)
            for s in range(NS):
                pe.wait_ge(roped, s + 1)
                for m in range(2):
                    last = nc.tensor.transpose(bank[6][:, m * SLOTS + s * P:m * SLOTS + (s + 1) * P],
                                               qk[:, s, m * H:(m + 1) * H, :, :].rearrange("p h two j -> p (h two j)"),
                                               sh.ident[:, :])
            last.then_inc(qk_turned, 1)

            def score(h):
                pe.wait_ge(qkT_done, h + 1)
                if h >= 2:
                    pe.wait_ge(masked, h - 1)
                for s in range(NS):
                    last = nc.tensor.matmul(bank[h % 2][:, s * SLOTS:s * SLOTS + SEL], qT[:, h, s * P:(s + 1) * P],
                                            kT[:, 0:SEL], start=True, stop=True)
                last.then_inc(scored, 1)

            def turn_probs(h):
                pe.wait_ge(exped, h + 1)
                if h >= 2:
                    pe.wait_ge(probT_done, h - 1)
                for k in range(NS):
                    for s in range(NS):
                        last = nc.tensor.transpose(bank[2 + h % 2][0:SELS[k], k * SLOTS + s * P:k * SLOTS + (s + 1) * P],
                                                   prob[:, h, s, k * P:k * P + SELS[k]], sh.ident[:, :])
                last.then_inc(prob_turned, 1)

            def weigh(h):
                pe.wait_ge(probT_done, h + 1)
                for s in range(NS):
                    for k in range(NS):
                        last = nc.tensor.matmul(bank[4][:, s * D + h * HD0:s * D + (h + 1) * HD0],
                                                probT[0:SELS[k], h % 4, k, s * P:(s + 1) * P],
                                                vs[0:SELS[k], k, h * HD0:(h + 1) * HD0],
                                                start=(k == 0), stop=(k == NS - 1))
                last.then_inc(weighted, 1)

            for h in range(H + 4):
                if h < H:
                    score(h)
                if 2 <= h < H + 2:
                    turn_probs(h - 2)
                if h >= 4:
                    weigh(h - 4)
            pe.wait_ge(o_done, 1)
            for s in range(NS):
                last = nc.tensor.transpose(bank[5][:, s * P:(s + 1) * P], o[:, s, :], sh.ident[:, :])
            last.then_inc(o_turned, 1)
            pe.wait_ge(oT_done, 1)
            for s in range(NS):
                last = nc.tensor.matmul(bank[6][:, s * D:(s + 1) * D], oT[:, s * P:(s + 1) * P], w_att[:, 3, :],
                                        start=True, stop=True)
            last.then_inc(mixed, 1)
            turn_hn(1, bank[7])
            pe.wait_ge(mlp_loaded, 32)
            for f in range(FT):
                last = nc.tensor.matmul(bank[f // 2][:, (f % 2) * SLOTS:(f % 2 + 1) * SLOTS], w1[:, f * P:(f + 1) * P],
                                        hnT[:, :], start=True, stop=True)
            last.then_inc(hidden, 1)
            pe.wait_ge(gated, 1)
            for s in range(NS):
                for f in range(FT):
                    last = nc.tensor.matmul(bank[4][:, s * D:(s + 1) * D],
                                            gate[:, 2, f * SLOTS + s * P:f * SLOTS + (s + 1) * P], w2[:, f, :],
                                            start=(f == 0), stop=(f == FT - 1))
            last.then_inc(downed, 1)
            pe.wait_ge(proc_done, NS)
            for t in range(T):
                for s in range(NS):
                    last = nc.tensor.matmul(bank[t // TC][:, (t % TC) * P:(t % TC + 1) * P],
                                            onehotT[0:SELS[s], s, t * P:(t + 1) * P], proc[0:SELS[s], s, :],
                                            start=(s == 0), stop=(s == NS - 1))
                if t % TC == TC - 1:
                    last.then_inc(scattered, 1)


def join0(nc, a, sh):
    with ExitStack() as ctx:
        def sb(name, shape, dt=F32):
            return ctx.enter_context(nc.sbuf_tensor(name, shape, dt))

        def sem(name):
            return ctx.enter_context(nc.semaphore(name))

        w_out = sb("w_out", [P, D])
        rows = sb("rows", [P, 3, D])
        oT = sb("o0T", [P, S])
        y = sb("y", [P, T, D])
        stats = sb("stats_j", [P, T, 6])
        moments = sb("moments_j", [P, T, 2])
        var_eps = sb("var_eps_j", [P, 2, T])
        root = sb("root_j", [P, 2, T])
        rstd = sb("rstd_j", [P, 2, T])
        newton = sb("newton_j", [P, T])

        w_loaded = sem("w_out_loaded")
        turned = sem("o0_turned")
        oT_done = sem("o0T_done")
        projected = sem("o0_projected")
        var_done = sem("var_done_j")
        root_done = sem("root_done_j")
        normed = sem("normed_j")
        xn_turned = sem("xn_turned_j")
        xnT_done = sem("xnT_done_j")
        step = sem("join_step")
        bank = sh.bank

        block = ctx.enter_context(nc.Block())

        @block.sync
        def _(sp):
            sp.dma_start(w_out[:, :], a["L0_attn_w_out"]).then_inc(w_loaded, 16)
            for n, name in enumerate(("b_out", "gamma", "beta")):
                sp.dma_start(rows[:, n, :], a["L0_attn_" + name].partition_broadcast(P)).then_inc(w_loaded, 16)

        @block.tensor
        def _(pe):
            for c in range(NC):
                for j in range(TC):
                    last = nc.tensor.transpose(bank[c][:, j * P:(j + 1) * P],
                                               sh.o0[:, c * TC + j, :, :].rearrange("p h j -> p (h j)"),
                                               sh.ident[:, :])
                last.then_inc(turned, 1)
            pe.wait_ge(w_loaded, 64)
            for c in range(NC):
                pe.wait_ge(oT_done, c + 1)
                for j in range(TC):
                    t = c * TC + j
                    last = nc.tensor.matmul(bank[4 + c][:, j * P:(j + 1) * P], oT[:, t * P:(t + 1) * P], w_out[:, :],
                                            start=True, stop=True)
                last.then_inc(projected, 1)
            for c in range(NC):
                pe.wait_ge(normed, (c + 1) * TC)
                for j in range(TC):
                    last = nc.tensor.transpose(bank[c][:, j * P:(j + 1) * P], sh.xa[:, c * TC + j, 0:D], sh.ident[:, :])
                last.then_inc(xn_turned, 1)

        @block.scalar
        def _(act):
            for c in range(NC):
                act.wait_ge(turned, c + 1)
                nc.scalar.copy(oT[:, c * C:(c + 1) * C], bank[c]).then_inc(oT_done, 1)
            for n in range(2):
                act.wait_ge(var_done, n + 1)
                nc.scalar.activation(root[:, n, :], var_eps[:, n, :], ACT.Sqrt).then_inc(root_done, 1)
            for c in range(NC):
                act.wait_ge(xn_turned, c + 1)
                nc.scalar.copy(sh.xnT[:, c * C:(c + 1) * C], bank[c]).then_inc(xnT_done, 1)

        @block.vector
        def _(dve):
            link = Chain(dve, step)

            def moments_of(n, src):
                for t in range(T):
                    last = nc.vector.bn_stats(stats[:, t, :], src[:, t, :])
                link(last)
                for t in range(T):
                    last = nc.vector.bn_aggr(moments[:, t, :], stats[:, t, :])
                link(last)
                nc.vector.tensor_scalar(var_eps[:, n, :], moments[:, :, 1], LN_EPS, None, ALU.add)\
                    .then_inc(var_done, 1)
                dve.wait_ge(root_done, n + 1)
                rsqrt_refine(link, nc, rstd[:, n, :], root[:, n, :], var_eps[:, n, :], newton[:, :])

            def row(n):
                return rows[:, n:n + 1, :].to_broadcast([P, T, D])

            dve.wait_ge(w_loaded, 64)
            for c in range(NC):
                at = slice(c * TC, (c + 1) * TC)
                dve.wait_ge(projected, c + 1)
                last = nc.vector.tensor_tensor(y[:, at, :], bank[4 + c].rearrange("p (t d) -> p t d", d=D),
                                               sh.xa[:, at, 0:D], ALU.add)
            link(last)
            link(nc.vector.tensor_tensor(y[:, :, :], y[:, :, :], row(0), ALU.add))
            moments_of(0, y)
            for t in range(T):
                last = nc.vector.tensor_scalar(y[:, t, :], y[:, t, :], moments[:, t, 0:1], rstd[:, 0, t:t + 1],
                                               ALU.subtract, ALU.mult)
            link(last)
            link(nc.vector.tensor_tensor(y[:, :, :], y[:, :, :], row(1), ALU.mult))
            link(nc.vector.tensor_tensor(y[:, :, :], y[:, :, :], row(2), ALU.add))
            link(nc.vector.tensor_tensor(y[:, :, :], y[:, :, :], sh.g[:, :, :], ALU.mult))
            link(nc.vector.tensor_tensor(sh.x[:, :, :], sh.x[:, :, :], y[:, :, :], ALU.add))
            moments_of(1, sh.x)
            for t in range(T):
                nc.vector.tensor_scalar(sh.xa[:, t, 0:D], sh.x[:, t, :], moments[:, t, 0:1], rstd[:, 1, t:t + 1],
                                        ALU.subtract, ALU.mult).then_inc(normed, 1)


def gated1(nc, a, sh):
    with ExitStack() as ctx:
        def sb(name, shape, dt=F32):
            return ctx.enter_context(nc.sbuf_tensor(name, shape, dt))

        def sem(name):
            return ctx.enter_context(nc.semaphore(name))

        w_int = sb("w_int", [P, 3, F1], I32)
        w_real = sb("w_real", [P, 3, F1])
        wT = sb("wT", [P, 3, F1])
        act_gate = sb("act_gate", [P, 2, C])
        inner = sb("inner", [P, F1T, S])

        w_loaded = sem("w1_loaded")
        w_scaled = sem("w1_scaled")
        w_turned = sem("w1_turned")
        wT_done = sem("w1T_done")
        gate_done = sem("gate1_done")
        gate_act = sem("gate1_act")
        inner_done = sem("inner1_done")
        down_done = sem("down1_done")
        g_done = sem("g1_done")
        bank = sh.bank

        block = ctx.enter_context(nc.Block())

        @block.sync
        def _(sp):
            for n, name in enumerate(("w_gate", "w_up")):
                sp.dma_start(w_int[:, n, :].rearrange("p (t d) -> p t d", d=D),
                             a["L1_ffn_" + name].rearrange("(t p) d -> p t d", p=P)).then_inc(w_loaded, 16)
            sp.dma_start(w_int[:, 2, :], a["L1_ffn_w_down"]).then_inc(w_loaded, 16)

        @block.tensor
        def _(pe):
            for n in range(3):
                pe.wait_ge(w_scaled, n + 1)
                for f in range(F1T):
                    last = nc.tensor.transpose(bank[n][:, f * P:(f + 1) * P], w_real[:, n, f * P:(f + 1) * P],
                                               sh.ident[:, :])
                last.then_inc(w_turned, 1)
            pe.wait_ge(wT_done, 3)
            for f in range(F1T):
                for c in range(NC):
                    n = f * NC + c
                    if n >= 2:
                        pe.wait_ge(inner_done, n - 1)
                    for m in range(2):
                        last = nc.tensor.matmul(bank[2 * (n % 2) + m], wT[:, m, f * P:(f + 1) * P],
                                                sh.xnT[:, c * C:(c + 1) * C], start=True, stop=True)
                    last.then_inc(gate_done, 1)
            pe.wait_ge(inner_done, F1T * NC)
            for c in range(NC):
                for j in range(TC):
                    t = c * TC + j
                    for f in range(F1T):
                        last = nc.tensor.matmul(bank[4 + c][:, j * P:(j + 1) * P], inner[:, f, t * P:(t + 1) * P],
                                                wT[:, 2, f * P:(f + 1) * P], start=(f == 0), stop=(f == F1T - 1))
                last.then_inc(down_done, 1)

        @block.scalar
        def _(act):
            for n in range(3):
                act.wait_ge(w_turned, n + 1)
                nc.scalar.copy(wT[:, n, :], bank[n][:, 0:F1]).then_inc(wT_done, 1)
            for n in range(F1T * NC):
                act.wait_ge(gate_done, n + 1)
                if n >= 2:
                    act.wait_ge(inner_done, n - 1)
                nc.scalar.activation(act_gate[:, n % 2, :], bank[2 * (n % 2)], ACT.Silu).then_inc(gate_act, 1)
            for c in range(NC):
                act.wait_ge(down_done, c + 1)
                nc.scalar.activation(sh.g[:, c * TC:(c + 1) * TC, :], bank[4 + c].rearrange("p (t d) -> p t d", d=D),
                                     ACT.Silu).then_inc(g_done, 1)

        @block.vector
        def _(dve):
            dve.wait_ge(w_loaded, 48)
            for n in range(3):
                nc.vector.tensor_scalar(w_real[:, n, :], w_int[:, n, :], Q_SCALE, None, ALU.mult).then_inc(w_scaled, 1)
            for n in range(F1T * NC):
                f, c = n // NC, n % NC
                dve.wait_ge(gate_act, n + 1)
                nc.vector.tensor_tensor(inner[:, f, c * C:(c + 1) * C], act_gate[:, n % 2, :], bank[2 * (n % 2) + 1],
                                        ALU.mult).then_inc(inner_done, 1)


def one(ap, n, axis):
    if isinstance(n, int):
        return ap[n] if axis == 0 else ap[:, n]
    if axis == 0:
        return ap[bass.ds(n, 1)].rearrange("o m d -> (o m) d")
    if len(ap.shape) == 3:
        return ap[:, bass.ds(n, 1), :].rearrange("p o m -> p (o m)")
    return ap[:, bass.ds(n, 1), :, :].rearrange("p o t d -> p (o t) d")


def column(bias, m, h, part):
    return bias[part, m, h:h + 1] if isinstance(h, int) else bias[part, m, bass.ds(h, 1)]


def attention1(nc, a, sh, out):
    with ExitStack() as ctx:
        def sb(name, shape, dt=F32):
            return ctx.enter_context(nc.sbuf_tensor(name, shape, dt))

        def sem(name):
            return ctx.enter_context(nc.semaphore(name))

        W = HD1
        PR = 4
        SCALE = 1.0 / math.sqrt(HD1)
        PAIRS = [(qc, j) for qc in range(NC) for j in range(2 * qc + 2)]
        NPAIR = len(PAIRS)
        PROJ = 2 * NC
        MAXES = [(i, c) for i in range(T) for c in range(i // TC + 1)]
        UNITS = PROJ + len(MAXES)
        SPREAD = NPAIR - 3
        DIAG = 2 * NC
        BODY = 2

        wq = [sb(f"wq{n}", [P, 2 * W]) for n in range(2)]
        wk = [sb(f"wk{n}", [P, 2 * W]) for n in range(2)]
        wo = sb("wo", [P, H, D])
        bias = sb("bias", [P, 2, H])
        row_o = sb("row_o", [P, D])
        q_hi = [sb(f"q_hi{n}", [P, S], F32R) for n in range(2)]
        k_both = [sb(f"k_both{n}", [P, S], F32R) for n in range(2)]
        q_lo = [sb(f"q_lo{n}", [P, S], F32R) for n in range(2)]
        k_hi = [sb(f"k_hi{n}", [P, S], F32R) for n in range(2)]
        k_tmp = sb("k_tmp", [P, C], F32R)
        causal = sb("causal", [P, P], BF16)
        ident_b = sb("ident_b", [P, P], BF16)
        v_all = sb("v_all", [P, H, T, W])
        v_head = [sb(f"v_head{n}", [P, T, W]) for n in range(2)]
        prob = sb("prob1", [P, PR, 2, C])
        acc = sb("acc", [P, 2, C])
        z = sb("z", [P, C])
        part_max = sb("part_max", [P, T, NC])
        neg_max = sb("neg_max", [P, T])
        inv = sb("inv", [P, TC])
        attn = sh.xa[:, :, 0:D]
        rows = prob[:, 0, :, :].rearrange("p m c -> p (m c)")
        bias_rows = acc[0:H, 0, 0:4 * W].rearrange("h (m w) -> h m w", m=2)
        wv = v_head[0][:, :, :].rearrange("p t d -> p (t d)")

        bias_loaded = sem("bias_loaded")
        wv_loaded = sem("wv_loaded")
        rows_loaded1 = sem("rows_loaded1")
        wo_loaded = sem("wo_loaded")
        qk_loaded = [sem(f"qk_loaded{n}") for n in range(2)]
        v_loaded = [sem(f"v_loaded{n}") for n in range(2)]
        consts_set = sem("consts1_set")
        pool_step = sem("pool1_step")
        bias_turned = sem("bias_turned")
        bias_done = sem("bias_done")
        v_projected = sem("v1_projected")
        v_done = sem("v1_done")
        prep_filled = sem("prep_filled")
        prep_freed = sem("prep_freed")
        act_split = sem("act_split")
        max_done = sem("max_done")
        max_turned = sem("max_turned")
        max_copied = sem("max_copied")
        part_step = sem("part_step")
        st_filled = sem("st_filled")
        exp_done = sem("exp_done")
        diag_masked = sem("diag_masked")
        weighted = sem("weighted1")
        summed = sem("summed")
        z_copied = sem("z_copied")
        mixed = sem("mixed1")
        inv_done = sem("inv_done")
        sum_done = sem("sum_done")
        added = sem("added")
        result_step = sem("result_step")
        act_passed = sem("act_passed")
        pool_passed = sem("pool_passed")
        result_done = sem("result_done")
        stored = sem("stored")

        bank = sh.bank
        st_slot = [sh.psum[:, 2 * n:2 * n + 2, :] for n in range(2)]
        prep_bank = bank[4:6]
        out_bank = bank[6]
        mix_bank = bank[7]

        block = ctx.enter_context(nc.Block())


        def first_column(qc, j):
            return max(0, 2 * j * P - qc * C)

        def units_of(n):
            return range(min(UNITS, UNITS * n // SPREAD), min(UNITS, UNITS * (n + 1) // SPREAD))

        def heads(engine, body):
            with engine.Fori(0, H // BODY - 1) as n:
                for p in range(BODY):
                    body(engine.snap(n * BODY + p), p, True)
            for p in range(BODY):
                body(H - BODY + p, p, p < BODY - 1)

        @block.sync
        def _(sp):
            for m, name in enumerate(("b_Q", "b_K")):
                for n in range(2):
                    sp.dma_start(bias_rows[:, m, n * W:(n + 1) * W], a["L1_attn_" + name]).then_inc(bias_loaded, 16)
            sp.dma_start(wv.rearrange("m (h d) -> m h d", d=W), a["L1_attn_W_V"].rearrange("h m d -> m h d"))\
                .then_inc(wv_loaded, 16)
            sp.dma_start(rows[:, :], a["L1_attn_b_V"].rearrange("h d -> (h d)").partition_broadcast(P))\
                .then_inc(rows_loaded1, 16)
            sp.dma_start(row_o[:, :], a["L1_attn_b_O"].partition_broadcast(P)).then_inc(rows_loaded1, 16)

            def load_qk(h, p):
                for tile, name in ((wq[p], "W_Q"), (wk[p], "W_K")):
                    for n in range(2):
                        sp.dma_start(tile[:, n * W:(n + 1) * W], one(a["L1_attn_" + name], h, 0))\
                            .then_inc(qk_loaded[p], 16)

            def load_v(h, p):
                sp.dma_start(v_head[p][:, :, :], one(v_all, h, 1)).then_inc(v_loaded[p], 16)

            for h in range(2):
                load_qk(h, h)
            for n in range(2):
                sp.dma_start(wo[n * W:(n + 1) * W, :, :], a["L1_attn_W_O"].rearrange("h d m -> d h m"))\
                    .then_inc(wo_loaded, 16)
            sp.wait_ge(v_done, 2 * T)
            for h in range(2):
                load_v(h, h)
            with sp.Fori(0, H // BODY - 1) as n:
                for p in range(BODY):
                    h = sp.snap(n * BODY + p)
                    sp.wait_ge(prep_filled, h * UNITS + PROJ)
                    load_qk(h + 2, p)
                    sp.wait_ge(weighted, (h + 1) * NPAIR + PR)
                    load_v(h + 2, p)
            for c in range(NC):
                sp.wait_ge(result_done, c + 1)
                sp.dma_start(out[0].rearrange("(t p) d -> p t d", p=P)[:, c * TC:(c + 1) * TC, :],
                             attn[:, c * TC:(c + 1) * TC, :]).then_inc(stored, 16)
            sp.wait_ge(stored, 16 * NC)

        @block.gpsimd
        def _(pool):
            pool.sem_inc(prep_freed, 2)
            pool.sem_inc(exp_done, 2)
            pool.sem_inc(weighted, PR)
            pool.sem_inc(summed, PR)
            pool.sem_inc(sum_done, 2)
            pool.sem_inc(mixed, 1)
            pool.sem_inc(inv_done, 1)
            pool.sem_inc(added, 1)
            link = Chain(pool, pool_step)
            link(nc.gpsimd.memset(causal[:, :], 0.0))
            link(nc.gpsimd.affine_select(out=causal[:, :], in_=causal[:, :], compare_op=ALU.is_ge, fill=NEG,
                                         base=0, pattern=[[-1, P]], channel_multiplier=1))
            link(nc.gpsimd.tensor_copy(ident_b[:, :], sh.ident[:, :]))
            for n in range(2):
                link(nc.gpsimd.memset(k_hi[n][W:W + 1, :].bitcast(F32), 1.0))
            nc.gpsimd.memset(part_max[:, :, :], -3.0e38).then_inc(consts_set, 1)

            def body(h, p, more):
                diag = 0
                for n, (qc, j) in enumerate(PAIRS):
                    q0 = first_column(qc, j)
                    pool.wait_ge(exp_done, h * NPAIR + (n + 3))
                    pair = prob[:, n % PR, :, :]
                    if j >= 2 * qc:
                        pool.sem_inc(pool_passed, 1)
                        wide = pair[:, :, q0:q0 + 2 * P]
                        nc.gpsimd.affine_select(out=wide, in_=wide, compare_op=ALU.is_ge, fill=0.0, base=0,
                                                pattern=[[-P, 2], [1, 2 * P]], channel_multiplier=-1)\
                            .then_inc(diag_masked, 1)
                        diag += 1
                        pool.wait_ge(diag_masked, h * DIAG + diag)
                    sums = acc[:, qc % 2, :]
                    if j == 0:
                        pool.wait_ge(sum_done, h * NC + (qc + 1))
                        nc.gpsimd.tensor_tensor(sums, pair[:, 0, :], pair[:, 1, :], ALU.add).then_inc(summed, 1)
                    else:
                        pool.wait_ge(summed, h * NPAIR + (n + PR))
                        nc.gpsimd.tensor_tensor(sums[:, q0:C], sums[:, q0:C], pair[:, 0, q0:C], ALU.add)\
                            .then_inc(part_step, 1)
                        pool.wait_ge(part_step, h * (NPAIR - NC) + (n - qc))
                        nc.gpsimd.tensor_tensor(sums[:, q0:C], sums[:, q0:C], pair[:, 1, q0:C], ALU.add)\
                            .then_inc(summed, 1)

            heads(pool, body)

        @block.tensor
        def _(pe):
            pe.wait_ge(bias_loaded, 64)
            for m in range(2):
                last = nc.tensor.transpose(mix_bank[:, m * H:(m + 1) * H], bias_rows[:, m, :], sh.ident[0:H, 0:H])
            last.then_inc(bias_turned, 1)
            pe.wait_ge(wv_loaded, 16)
            for t in range(T):
                for n in range(2):
                    u = 2 * t + n
                    if u >= 2:
                        pe.wait_ge(v_done, u - 1)
                    nc.tensor.matmul(prep_bank[n], sh.xnT[:, t * P:(t + 1) * P], wv[:, n * C:(n + 1) * C],
                                     start=True, stop=True).then_inc(v_projected, 1)
            pe.wait_ge(v_done, 2 * T)
            pe.wait_ge(consts_set, 1)
            pe.wait_ge(bias_done, 1)

            def prepare_unit(h, p, u):
                pe.wait_ge(prep_freed, h * UNITS + (u + 1))
                to = prep_bank[u % 2]
                if u < PROJ:
                    c = u // 2
                    last = nc.tensor.matmul(to, (wq if u % 2 == 0 else wk)[p][:, :], sh.xnT[:, c * C:(c + 1) * C],
                                            start=True, stop=True)
                else:
                    if u == PROJ:
                        pe.wait_ge(prep_freed, h * UNITS + (PROJ + 2))
                    i, c = MAXES[u - PROJ]
                    n = min(C, (i + 1) * P - c * C)
                    diagonal = c == i // TC
                    last = nc.tensor.matmul(to[:, 0:n], q_hi[p][:, i * P:(i + 1) * P], k_both[p][:, c * C:c * C + n],
                                            start=True, stop=not diagonal)
                    if diagonal:
                        last = nc.tensor.matmul(to[:, n - P:n], ident_b[:, :], causal[:, :], start=False, stop=True)
                last.then_inc(prep_filled, 1)

            def turn_max(h):
                pe.wait_ge(max_done, h + 1)
                for c in range(NC):
                    if c >= 2:
                        pe.wait_ge(max_copied, h * NC + (c - 1))
                    for j in range(TC):
                        t = c * TC + j
                        last = nc.tensor.transpose(prep_bank[c % 2][0:1, j * P:(j + 1) * P], neg_max[:, t:t + 1],
                                                   sh.ident[:, :])
                    last.then_inc(max_turned, 1)

            def score(h, p, n):
                qc, j = PAIRS[n]
                q0 = first_column(qc, j)
                at = slice(qc * C + q0, (qc + 1) * C)
                pe.wait_ge(exp_done, h * NPAIR + (n + 1))
                for m in range(2):
                    kt = slice((2 * j + m) * P, (2 * j + m + 1) * P)
                    to = st_slot[n % 2][:, m, q0:C]
                    nc.tensor.matmul(to, k_both[p][:, kt], q_hi[p][:, at], start=True, stop=False)
                    last = nc.tensor.matmul(to, k_hi[p][0:W + 1, kt], q_lo[p][0:W + 1, at], start=False, stop=True)
                last.then_inc(st_filled, 1)

            def weigh(h, p, n):
                qc, j = PAIRS[n]
                q0 = first_column(qc, j)
                if j >= 2 * qc:
                    pe.wait_ge(diag_masked, h * DIAG + (2 * qc + j - 2 * qc + 1))
                else:
                    pe.wait_ge(exp_done, h * NPAIR + (n + 3))
                if j == 0:
                    pe.wait_ge(inv_done, h * NC + (qc + 1))
                for m in range(2):
                    last = nc.tensor.matmul(out_bank[m * W:(m + 1) * W, q0:C], v_head[p][:, 2 * j + m, :],
                                            prob[:, n % PR, m, q0:C], start=(j == 0), stop=(j == 2 * qc + 1))
                last.then_inc(weighted, 1)

            def mix(h, qc):
                turn = h * NC + qc
                pe.wait_ge(z_copied, turn + 1)
                pe.wait_ge(summed, h * NPAIR + ((qc + 1) * (qc + 2) + PR))
                for j in range(TC):
                    last = nc.tensor.matmul(out_bank[:, j:j + 1], acc[:, qc % 2, j * P:(j + 1) * P], sh.ones[:, 0:1],
                                            start=True, stop=True)
                last.then_inc(sum_done, 1)
                pe.wait_ge(added, turn + 1)
                for j in range(TC):
                    last = nc.tensor.matmul(mix_bank[:, j * P:(j + 1) * P], z[:, j * P:(j + 1) * P], one(wo, h, 1),
                                            start=True, stop=True)
                last.then_inc(mixed, 1)

            pe.wait_ge(qk_loaded[0], 64)
            for u in range(UNITS):
                prepare_unit(0, 0, u)
            turn_max(0)
            pe.wait_ge(wo_loaded, 32)

            def body(h, p, more):
                if more:
                    pe.wait_ge(qk_loaded[1 - p], (h + (p + 2)) * 32)
                pe.wait_ge(max_copied, (h + 1) * NC)
                pe.wait_ge(v_loaded[p], (h + (2 - p)) * 8)
                for n, (qc, j) in enumerate(PAIRS):
                    score(h, p, n)
                    if more:
                        for u in units_of(n):
                            prepare_unit(h + 1, 1 - p, u)
                    if more and n == SPREAD:
                        turn_max(h + 1)
                    if j == 1 and qc > 0:
                        mix(h, qc - 1)
                    if n > 0:
                        weigh(h, p, n - 1)
                weigh(h, p, NPAIR - 1)
                mix(h, NC - 1)

            heads(pe, body)

        @block.scalar
        def _(act):
            act.wait_ge(bias_turned, 1)
            nc.scalar.copy(bias[:, :, :], mix_bank[:, 0:2 * H].rearrange("p (m h) -> p m h", m=2)).then_inc(bias_done, 1)
            act.wait_ge(bias_done, 1)

            def split(h, p, u):
                c = u // 2
                at = slice(c * C, (c + 1) * C)
                act.wait_ge(prep_filled, h * UNITS + (u + 1))
                act.sem_inc(act_passed, 1)
                src = prep_bank[u % 2]
                whole, top, low = slice(0, P), slice(0, W), slice(W, P)
                if u % 2 == 0:
                    nc.scalar.activation(q_hi[p][:, at], src, ACT.Identity, bias=column(bias, 0, h, whole))\
                        .then_inc(act_split, 1)
                else:
                    nc.scalar.activation(k_both[p][top, at], src[top, :], ACT.Identity, bias=column(bias, 1, h, top))
                    nc.scalar.activation(k_hi[p][top, at], src[top, :], ACT.Identity, bias=column(bias, 1, h, top))
                    if c:
                        act.wait_ge(prep_freed, h * UNITS + (u + 1))
                        act.sem_inc(act_passed, 1)
                    nc.scalar.activation(k_tmp[low, :], src[low, :], ACT.Identity, bias=column(bias, 1, h, low))\
                        .then_inc(act_split, 1)

            def copy_max(h, p):
                for c in range(NC):
                    act.wait_ge(max_turned, h * NC + (c + 1))
                    nc.scalar.copy(q_lo[p][W:W + 1, c * C:(c + 1) * C], prep_bank[c % 2][0:1, :])\
                        .then_inc(max_copied, 1)

            for u in range(PROJ):
                split(0, 0, u)
            copy_max(0, 0)

            def body(h, p, more):
                for n, (qc, j) in enumerate(PAIRS):
                    q0 = first_column(qc, j)
                    act.wait_ge(st_filled, h * NPAIR + (n + 1))
                    act.wait_ge(weighted, h * NPAIR + (n + 1))
                    act.wait_ge(summed, h * NPAIR + (n + 1))
                    nc.scalar.activation(prob[:, n % PR, :, q0:C], st_slot[n % 2][:, :, q0:C], ACT.Exp, scale=SCALE)\
                        .then_inc(exp_done, 1)
                    if more:
                        for u in units_of(n):
                            if u < PROJ:
                                split(h + 1, 1 - p, u)
                    if more and n == SPREAD:
                        copy_max(h + 1, 1 - p)

            heads(act, body)

        @block.vector
        def _(dve):
            link = Chain(dve, result_step)
            dve.wait_ge(rows_loaded1, 32)
            for t in range(T):
                for n in range(2):
                    u = 2 * t + n
                    dve.wait_ge(v_projected, u + 1)
                    half = slice(n * H // 2, (n + 1) * H // 2)
                    nc.vector.tensor_tensor(v_all[:, half, t, :], prep_bank[n].rearrange("p (h d) -> p h d", d=W),
                                            rows[:, n * C:(n + 1) * C].rearrange("p (h d) -> p h d", d=W), ALU.add)\
                        .then_inc(v_done, 1)
            link(nc.vector.tensor_copy(attn[:, :, :], row_o[:, :].unsqueeze(1).to_broadcast([P, T, D])))
            dve.wait_ge(consts_set, 1)
            dve.wait_ge(bias_done, 1)

            def consume(h, p, u):
                src = prep_bank[u % 2]
                if u < PROJ:
                    c = u // 2
                    at = slice(c * C, (c + 1) * C)
                    dve.wait_ge(act_split, h * PROJ + (u + 1))
                    part, lo, hi = ((slice(0, W), q_lo[p][0:W, at], q_hi[p][0:W, at]) if u % 2 == 0 else
                                    (slice(W, P), k_both[p][W:P, at], k_tmp[W:P, :]))
                    nc.vector.scalar_tensor_tensor(out=lo, in0=src[part, :], scalar=column(bias, u % 2, h, part),
                                                   in1=hi.bitcast(F32), op0=ALU.add, op1=ALU.subtract)\
                        .then_inc(prep_freed, 1)
                else:
                    i, c = MAXES[u - PROJ]
                    n = min(C, (i + 1) * P - c * C)
                    dve.wait_ge(prep_filled, h * UNITS + (u + 1))
                    nc.vector.tensor_reduce(part_max[:, i, c:c + 1], src[:, 0:n], AX_X, ALU.max)\
                        .then_inc(prep_freed, 1)
                    if u == UNITS - 1:
                        dve.wait_ge(prep_freed, (h + 1) * UNITS + 2)
                        if not (isinstance(h, int) and h == 0):
                            dve.wait_ge(max_turned, h * NC)
                        nc.vector.tensor_reduce(neg_max[:, :], part_max[:, :, :], AX_X, ALU.max, negate=True)\
                            .then_inc(max_done, 1)

            def copy_out(h, qc):
                turn = h * NC + qc
                dve.wait_ge(weighted, h * NPAIR + ((qc + 1) * (qc + 2) + PR))
                dve.wait_ge(mixed, turn + 1)
                nc.vector.tensor_copy(z[:, :], out_bank).then_inc(z_copied, 1)

            def add(h, qc):
                turn = h * NC + qc
                dve.wait_ge(sum_done, turn + 3)
                nc.vector.reciprocal(inv[:, :], out_bank[:, 0:TC]).then_inc(inv_done, 1)
                dve.wait_ge(inv_done, turn + 2)
                dve.wait_ge(mixed, turn + 2)
                for j in range(TC):
                    t = qc * TC + j
                    last = nc.vector.scalar_tensor_tensor(out=attn[:, t, :], in0=mix_bank[:, j * P:(j + 1) * P],
                                                          scalar=inv[:, j:j + 1], in1=attn[:, t, :],
                                                          op0=ALU.mult, op1=ALU.add)
                last.then_inc(added, 1)

            for u in range(UNITS):
                consume(0, 0, u)

            def body(h, p, more):
                for n, (qc, j) in enumerate(PAIRS):
                    if j == 1 and qc > 0:
                        copy_out(h, qc - 1)
                    if more:
                        for u in units_of(n):
                            consume(h + 1, 1 - p, u)
                    if j == 1 and qc > 0:
                        add(h, qc - 1)
                copy_out(h, NC - 1)
                add(h, NC - 1)

            heads(dve, body)
            dve.wait_ge(added, H * NC + 1)
            for c in range(NC):
                at = slice(c * TC, (c + 1) * TC)
                link(nc.vector.tensor_tensor(attn[:, at, :], attn[:, at, :], sh.g[:, at, :], ALU.mult))
                nc.vector.tensor_tensor(attn[:, at, :], attn[:, at, :], sh.x[:, at, :], ALU.add)\
                    .then_inc(result_done, 1)


INPUTS = [
    "L0_attn_x", "L0_attn_w_qkv", "L0_attn_w_out", "L0_attn_b_out", "L0_attn_gamma", "L0_attn_beta",
    "L0_ffn_attention_mask", "L0_ffn_position_ids", "L0_ffn_router_w", "L0_ffn_router_b", "L0_ffn_wq", "L0_ffn_wk",
    "L0_ffn_wv", "L0_ffn_wo", "L0_ffn_w1", "L0_ffn_w2", "L0_ffn_ln1", "L0_ffn_ln2",
    "L1_attn_W_Q", "L1_attn_W_K", "L1_attn_W_V", "L1_attn_W_O", "L1_attn_b_Q", "L1_attn_b_K", "L1_attn_b_V",
    "L1_attn_b_O", "L1_ffn_w_gate", "L1_ffn_w_up", "L1_ffn_w_down",
]


def build(nc, a, out):
    with ExitStack() as ctx:
        sh = Shared()

        def sb(name, shape, dt=F32):
            return ctx.enter_context(nc.sbuf_tensor(name, shape, dt))

        sh.x = sb("x", [P, T, D])
        sh.xa = sb("xa", [P, T, D + 2])
        sh.xnT = sb("xnT", [P, S])
        sh.g = sb("g", [P, T, D])
        sh.ident = sb("ident", [P, P])
        sh.ones = sb("ones", [P, P])
        sh.psum = ctx.enter_context(nc.psum_tensor("psum", [P, 8, C], F32))
        sh.bank = [sh.psum[:, b, :] for b in range(8)]
        sh.parts_dram = nc.dram_tensor("parts_dram", [2, PARTS, D, S], BF16, kind="Internal").ap()
        with ExitStack() as layer0:
            sh.v0 = layer0.enter_context(nc.sbuf_tensor("v0", [P, T, D], F32))
            sh.o0 = layer0.enter_context(nc.sbuf_tensor("o0", [P, T, H, HD0], F32))
            prepare(nc, a, sh)
            routed0(nc, a, sh)
            attention0(nc, a, sh)
            join0(nc, a, sh)
        gated1(nc, a, sh)
        attention1(nc, a, sh, out)


def kernel(**inputs):
    import concourse.bacc as bacc
    from concourse.bass_utils import run_bass_kernel_spmd

    nc = bacc.Bacc("TRN2", target_bir_lowering=False, num_devices=1)
    arrays, a = {}, {}
    for name in INPUTS:
        array = np.ascontiguousarray(inputs[name])
        arrays["in_" + name] = array
        a[name] = nc.dram_tensor("in_" + name, array.shape, mybir.dt.from_np(array.dtype), kind="ExternalInput").ap()
    out = nc.dram_tensor("out", (1, S, D), F32, kind="ExternalOutput").ap()
    build(nc, a, out)
    result = run_bass_kernel_spmd(nc, [arrays], core_ids=[0])
    return result.results[0]["out"]
```

```python
from contextlib import ExitStack
import math

import numpy as np
import concourse.bass as bass
from concourse import mybir

F32 = mybir.dt.float32
F32R = mybir.dt.float32r
BF16 = mybir.dt.bfloat16
I32 = mybir.dt.int32
ALU = mybir.AluOpType
ACT = mybir.ActivationFunctionType
AX_X = mybir.AxisListType.X

P = 128
S = 2048
D = 128
T = S // P
C = 512
NC = S // C
TC = C // P
H = 16
HD0 = D // H
PARTS = 3
ROWS0 = PARTS * PARTS * HD0
GH = 4
G = H // GH
VW = 32
LOADS = 2 * PARTS * PARTS
LN_EPS = 1e-5
KERN_EPS = 1e-6
RMS_EPS = 1e-6
SEL = S // 8 - 1
SLOTS = SEL + 1
NS = SLOTS // P
SELS = [P, SEL - P]
MP = 512
MT = MP // P
F0 = 512
FT = F0 // P
HD1 = 64
F1 = 384
F1T = F1 // P
Q_SCALE = 1.0 / 127.0
NEG = -1e30
EXP_MAX = 80.0


class Chain:

    def __init__(self, engine, semaphore):
        self.engine, self.semaphore, self.steps = engine, semaphore, 0

    def __call__(self, instruction):
        instruction.then_inc(self.semaphore, 1)
        self.steps += 1
        self.engine.wait_ge(self.semaphore, self.steps)


def rsqrt_refine(link, nc, out, root, square, work):
    link(nc.vector.reciprocal(out, root))
    link(nc.vector.tensor_tensor(work, out, out, ALU.mult))
    link(nc.vector.tensor_tensor(work, work, square, ALU.mult))
    link(nc.vector.tensor_scalar(work, work, -0.5, 1.5, ALU.mult, ALU.add))
    link(nc.vector.tensor_tensor(out, out, work, ALU.mult))


class Shared:
    pass


def prepare(nc, a, sh):
    with ExitStack() as ctx:
        def sb(name, shape, dt=F32):
            return ctx.enter_context(nc.sbuf_tensor(name, shape, dt))

        def sem(name):
            return ctx.enter_context(nc.semaphore(name))

        wqkv = sb("wqkv", [P, 3 * D])
        w_parts = sb("w_parts", [P, 3, D])
        stats = sb("stats", [P, T, 6])
        moments = sb("moments", [P, T, 2])
        var_eps = sb("var_eps", [P, T])
        root = sb("root", [P, T])
        rstd = sb("rstd", [P, T])
        newton = sb("newton", [P, T])
        parts = sb("parts", [P, 2, PARTS, S], BF16)
        rest = sb("rest", [P, 2, 2, C])

        x_loaded = [sem(f"x_loaded{c}") for c in range(NC)]
        w_loaded = sem("w_loaded")
        w_parted = sem("w_parted")
        ident_zero = sem("ident_zero")
        ident_done = sem("ident_done")
        var_done = sem("var_done")
        root_done = sem("root_done")
        norm_step = sem("norm_step")
        normed = sem("normed")
        turned = sem("turned")
        turned_out = sem("turned_out")
        projected = sem("projected")
        part1_done = sem("part1_done")
        rest1_done = sem("rest1_done")
        part2_done = sem("part2_done")
        part3_done = sem("part3_done")
        v_projected = sem("v_projected")
        v_out = sem("v_out")
        parts_stored = sem("parts_stored")
        cs_done = sem("cs_done")

        x_view = a["L0_attn_x"][0].rearrange("(t p) d -> p t d", p=P)
        bank = sh.bank

        block = ctx.enter_context(nc.Block())

        @block.sync
        def _(sp):
            for c in range(NC):
                sp.dma_start(sh.x[:, c * TC:(c + 1) * TC, :], x_view[:, c * TC:(c + 1) * TC, :])\
                    .then_inc(x_loaded[c], 16)
            sp.dma_start(wqkv[:, :], a["L0_attn_w_qkv"]).then_inc(w_loaded, 16)
            for m in range(2):
                for n in range(PARTS):
                    last = [part1_done, part2_done, part3_done][n]
                    sp.wait_ge(last, NC * (m + 1))
                    sp.dma_start(sh.parts_dram[m, n], parts[:, m, n, :]).then_inc(parts_stored, 16)
            sp.wait_ge(parts_stored, 16 * 2 * PARTS)

        @block.gpsimd
        def _(pool):
            nc.gpsimd.memset(sh.ident[:, :], 0.0).then_inc(ident_zero, 1)
            nc.gpsimd.memset(sh.ones[:, :], 1.0).then_inc(cs_done, 1)
            pool.wait_ge(ident_zero, 1)
            nc.gpsimd.affine_select(out=sh.ident[:, :], in_=sh.ident[:, :], compare_op=ALU.not_equal, fill=1.0,
                                    base=0, pattern=[[-1, P]], channel_multiplier=1).then_inc(ident_done, 1)
            pool.wait_ge(w_loaded, 16)
            for m in range(3):
                nc.gpsimd.tensor_copy(w_parts[:, m, :].rearrange("d (h j) -> d h j", j=HD0),
                                      wqkv[:, :].rearrange("d (h c j) -> d c h j", c=3, j=HD0)[:, m])\
                    .then_inc(w_parted, 1)

        @block.vector
        def _(dve):
            link = Chain(dve, norm_step)
            for t in range(T):
                if t % TC == 0:
                    dve.wait_ge(x_loaded[t // TC], 16)
                stat = nc.vector.bn_stats(stats[:, t, :], sh.x[:, t, :])
            link(stat)
            for t in range(T):
                last = nc.vector.bn_aggr(moments[:, t, :], stats[:, t, :])
            link(last)
            nc.vector.tensor_scalar(var_eps[:, :], moments[:, :, 1], LN_EPS, None, ALU.add).then_inc(var_done, 1)
            dve.wait_ge(root_done, 1)
            rsqrt_refine(link, nc, rstd[:, :], root[:, :], var_eps[:, :], newton[:, :])
            for t in range(T):
                nc.vector.tensor_scalar(sh.xa[:, t, 0:D], sh.x[:, t, :], moments[:, t, 0:1], rstd[:, t:t + 1],
                                        ALU.subtract, ALU.mult).then_inc(normed, 1)
            for n in range(2 * NC):
                m, c = n // NC, n % NC
                at = slice(c * C, (c + 1) * C)
                dve.wait_ge(part1_done, n + 1)
                if n >= 2:
                    dve.wait_ge(part3_done, n - 1)
                nc.vector.tensor_tensor(rest[:, n % 2, 0, :], bank[4 + n % 2], parts[:, m, 0, at],
                                        ALU.subtract).then_inc(rest1_done, 1)
                dve.wait_ge(part2_done, n + 1)
                nc.vector.tensor_tensor(parts[:, m, 2, at], rest[:, n % 2, 0, :], parts[:, m, 1, at],
                                        ALU.subtract).then_inc(part3_done, 1)
            for c in range(NC):
                dve.wait_ge(v_projected, c + 1)
                nc.vector.tensor_copy(sh.v0[:, c * TC:(c + 1) * TC, :],
                                      bank[6 + c % 2].rearrange("p (t d) -> p t d", d=D)).then_inc(v_out, 1)

        @block.scalar
        def _(act):
            act.wait_ge(var_done, 1)
            nc.scalar.activation(root[:, :], var_eps[:, :], ACT.Sqrt).then_inc(root_done, 1)
            for c in range(NC):
                act.wait_ge(turned, c + 1)
                nc.scalar.copy(sh.xnT[:, c * C:(c + 1) * C], bank[c]).then_inc(turned_out, 1)
            for n in range(2 * NC):
                m, c = n // NC, n % NC
                at = slice(c * C, (c + 1) * C)
                act.wait_ge(projected, n + 1)
                nc.scalar.copy(parts[:, m, 0, at], bank[4 + n % 2]).then_inc(part1_done, 1)
                act.wait_ge(rest1_done, n + 1)
                nc.scalar.copy(parts[:, m, 1, at], rest[:, n % 2, 0, :]).then_inc(part2_done, 1)

        @block.tensor
        def _(pe):
            pe.wait_ge(ident_done, 1)
            for t in range(T):
                pe.wait_ge(normed, t + 1)
                last = nc.tensor.transpose(bank[t // TC][:, (t % TC) * P:(t % TC + 1) * P], sh.xa[:, t, 0:D],
                                           sh.ident[:, :])
                if t % TC == TC - 1:
                    last.then_inc(turned, 1)
            pe.wait_ge(w_parted, 3)
            for n in range(2 * NC):
                m, c = n // NC, n % NC
                pe.wait_ge(turned_out, c + 1)
                if n >= 2:
                    pe.wait_ge(rest1_done, n - 1)
                nc.tensor.matmul(bank[4 + n % 2], w_parts[:, m, :], sh.xnT[:, c * C:(c + 1) * C],
                                 start=True, stop=True).then_inc(projected, 1)
            for c in range(NC):
                if c >= 2:
                    pe.wait_ge(v_out, c - 1)
                for j in range(TC):
                    t = c * TC + j
                    last = nc.tensor.matmul(bank[6 + c % 2][:, j * P:(j + 1) * P], sh.xnT[:, t * P:(t + 1) * P],
                                            w_parts[:, 2, :], start=True, stop=True)
                last.then_inc(v_projected, 1)


def load_rows(sp, sh, group, q_rows, k_rows, loaded):
    heads = slice(group * GH * HD0, (group + 1) * GH * HD0)
    for n in range(PARTS):
        for r in range(PARTS):
            rows = slice((n * PARTS + r) * HD0, (n * PARTS + r + 1) * HD0)
            sp.dma_start(q_rows[rows, :, :], sh.parts_dram[0, n, heads, :].rearrange("(h j) s -> j h s", j=HD0))\
                .then_inc(loaded, 16)
            sp.dma_start(k_rows[rows, :, :], sh.parts_dram[1, r, heads, :].rearrange("(h j) s -> j h s", j=HD0))\
                .then_inc(loaded, 16)


def attention0(nc, a, sh):
    with ExitStack() as ctx:
        def sb(name, shape, dt=F32):
            return ctx.enter_context(nc.sbuf_tensor(name, shape, dt))

        def sem(name):
            return ctx.enter_context(nc.semaphore(name))

        WR = 4
        NB = 2
        ACT_HEADS = (0, 1)
        DVE_HEADS = (2, 3)
        q_rows = [sh.q_rows] + [sb(f"q_rows{n}", [P, GH, S], BF16) for n in range(1, NB)]
        k_rows = [sh.k_rows] + [sb(f"k_rows{n}", [P, GH, S], BF16) for n in range(1, NB)]
        v_cols = [sh.v_cols] + [sb(f"v_cols{n}", [P, T, GH, VW]) for n in range(1, NB)]
        w = sb("w0", [P, WR, GH, C])
        o_sb = sb("o_sb", [P, C])
        den = sb("den", [P, TC, GH])

        rows_loaded = [sh.rows_loaded] + [sem(f"rows_loaded{n}") for n in range(1, NB)]
        ring_zeroed = sem("ring_zeroed")
        v_copied = sem("v_copied")
        scored = sem("scored")
        act_relu = sem("act_relu")
        dve_relu = sem("dve_relu")
        weighted = sem("weighted")
        out_copied = sem("out_copied")
        out_turned = sem("out_turned")
        den_step = sem("den_step")
        out_done = sem("out_done")

        bank = sh.bank
        score_bank = bank[0:GH]
        out_bank = bank[4]
        turn_bank = bank[5]
        turn_view = turn_bank.rearrange("p (t h v) -> p t h v", t=TC, h=GH)

        block = ctx.enter_context(nc.Block())


        @block.sync
        def _(sp):
            for group in range(1, G):
                par = group % NB
                if group >= NB:
                    sp.wait_ge(scored, (group - NB + 1) * NC * T * GH)
                load_rows(sp, sh, group, q_rows[par], k_rows[par], rows_loaded[par])

        @block.gpsimd
        def _(pool):
            pool.sem_inc(weighted, WR - 1)
            pool.sem_inc(act_relu, len(ACT_HEADS))
            pool.sem_inc(dve_relu, len(DVE_HEADS))
            pool.sem_inc(out_turned, 1)
            pool.sem_inc(out_done, 1)
            pool.sem_inc(v_copied, 1)
            for n in range(1, NB):
                nc.gpsimd.memset(v_cols[n][:, :, :, HD0 + 1:VW], 0.0)
                nc.gpsimd.memset(v_cols[n][:, :, :, HD0:HD0 + 1], 1.0)
            for group in range(1, G):
                if group >= NB:
                    pool.wait_ge(weighted, WR + (group - NB + 1) * NC * T)
                heads = sh.v0[:, :, group * GH * HD0:(group + 1) * GH * HD0]
                nc.gpsimd.tensor_copy(v_cols[group % NB][:, :, :, 0:HD0],
                                      heads.rearrange("p t (h j) -> p t h j", j=HD0)).then_inc(v_copied, 1)

        @block.tensor
        def _(pe):
            def scores(par, done, kt, qc):
                for h in range(GH):
                    if h in ACT_HEADS:
                        pe.wait_ge(act_relu, (done + kt) * len(ACT_HEADS) + ACT_HEADS.index(h) + 1)
                    else:
                        pe.wait_ge(dve_relu, (done + kt) * len(DVE_HEADS) + DVE_HEADS.index(h) + 1)
                    nc.tensor.matmul(score_bank[h], k_rows[par][0:ROWS0, h, kt * P:(kt + 1) * P],
                                     q_rows[par][0:ROWS0, h, bass.ds(qc * C, C)],
                                     start=True, stop=True).then_inc(scored, 1)

            def weigh(par, done, kt):
                if done is not None:
                    pe.wait_ge(act_relu, (done + kt + 2) * len(ACT_HEADS))
                    pe.wait_ge(dve_relu, (done + kt + 2) * len(DVE_HEADS))
                for h in range(GH):
                    last = nc.tensor.matmul(out_bank[h * VW:(h + 1) * VW, :], v_cols[par][:, kt, h, :],
                                            w[:, kt % WR, h, :], start=(kt == 0), stop=(kt == T - 1))
                last.then_inc(weighted, 1)

            def chunk(par, last_par, turn, qc):
                done = pe.snap(turn * T)
                scores(par, done, 0, qc)
                if isinstance(qc, int):
                    pe.wait_ge(v_copied, NB)
                weigh(last_par, None, T - 1)
                for kt in range(1, T):
                    scores(par, done, kt, qc)
                    if kt == 1:
                        pe.wait_ge(out_copied, turn + 1)
                    weigh(par, done, kt - 1)
                    if kt == 2:
                        turn_output(turn)

            def turn_output(turn):
                pe.wait_ge(out_copied, turn + 1)
                pe.wait_ge(out_done, turn + 1)
                for j in range(TC):
                    last = nc.tensor.transpose(turn_bank[:, j * P:(j + 1) * P], o_sb[:, j * P:(j + 1) * P],
                                               sh.ident[:, :])
                last.then_inc(out_turned, 1)

            pe.wait_ge(ring_zeroed, 1)
            for h in range(GH):
                nc.tensor.matmul(out_bank[h * VW:(h + 1) * VW, :], v_cols[0][:, 0, h, :], w[:, (T - 1) % WR, h, :],
                                 start=True, stop=False)
            with pe.Fori(0, G // NB) as pair:
                for par in range(NB):
                    pe.wait_ge(rows_loaded[par], (pair + 1) * (16 * LOADS))
                    pe.wait_ge(v_copied, pair * NB + (par + 1))
                    first = pe.snap(pair * (NB * NC) + par * NC)
                    chunk(par, 1 - par, first, 0)
                    with pe.Fori(1, NC) as qc:
                        chunk(par, par, pe.snap(first + qc), qc)
            pe.wait_ge(act_relu, (G * NC * T + 1) * len(ACT_HEADS))
            pe.wait_ge(dve_relu, (G * NC * T + 1) * len(DVE_HEADS))
            weigh((G - 1) % NB, None, T - 1)
            turn_output(G * NC)

        @block.scalar
        def _(act):
            def copy_out(turn):
                act.wait_ge(weighted, turn * T + WR)
                act.wait_ge(out_turned, turn + 1)
                nc.scalar.copy(o_sb[:, :], out_bank).then_inc(out_copied, 1)

            with act.Fori(0, G * NC) as turn:
                for kt in range(T):
                    act.wait_ge(weighted, turn * T + (kt + 1))
                    for h in ACT_HEADS:
                        act.wait_ge(scored, turn * (T * GH) + (kt * GH + h + 1))
                        nc.scalar.activation(w[:, kt % WR, h, :], score_bank[h], ACT.Relu).then_inc(act_relu, 1)
                    if kt == 0:
                        copy_out(turn)
            copy_out(G * NC)

        @block.vector
        def _(dve):
            def divide(turn):
                dve.wait_ge(out_turned, turn + 2)
                nc.vector.tensor_scalar(den[:, :, :], turn_view[:, :, :, HD0], KERN_EPS * math.sqrt(HD0), None,
                                        ALU.add).then_inc(den_step, 1)
                dve.wait_ge(den_step, turn * 2 + 1)
                nc.vector.reciprocal(den[:, :, :], den[:, :, :]).then_inc(den_step, 1)
                dve.wait_ge(den_step, turn * 2 + 2)
                to = sh.o0[:, turn, :, :] if isinstance(turn, int) else \
                    sh.o0[:, bass.ds(turn, 1), :, :].rearrange("p o t d -> p (o t) d")
                nc.vector.tensor_tensor(to.rearrange("p t (h j) -> p t h j", j=HD0), turn_view[:, :, :, 0:HD0],
                                        den[:, :, :].unsqueeze(3).to_broadcast([P, TC, GH, HD0]),
                                        ALU.mult).then_inc(out_done, 1)

            nc.vector.memset(w[:, (T - 1) % WR, :, :], 0.0).then_inc(ring_zeroed, 1)
            with dve.Fori(0, G * NC) as turn:
                for kt in range(T):
                    dve.wait_ge(weighted, turn * T + (kt + 1))
                    for h in DVE_HEADS:
                        dve.wait_ge(scored, turn * (T * GH) + (kt * GH + h + 1))
                        nc.vector.tensor_scalar(w[:, kt % WR, h, :], score_bank[h], 0.0, None, ALU.max)\
                            .then_inc(dve_relu, 1)
                    if kt == 3:
                        divide(turn)
            divide(G * NC)


def routed0(nc, a, sh):
    with ExitStack() as ctx:
        def sb(name, shape, dt=F32):
            return ctx.enter_context(nc.sbuf_tensor(name, shape, dt))

        def sem(name):
            return ctx.enter_context(nc.semaphore(name))

        TWO_PI = (6.28125, 0.0019350051879882812, 3.019916050561733e-07)
        ROUND = 1.5 * 2.0 ** 23
        HALF = HD0 // 2
        INV_FREQ = [float(f) for f in np.float32(1.0) / np.float32(10000.0) ** (
            np.arange(0, HD0, 2, dtype=np.float32) / np.float32(HD0))]

        router_b = sb("router_b", [P, D])
        bias_b = sb("bias_b", [P, 1])
        pos_own = sb("pos_own", [P, MT], I32)
        pos_last = sb("pos_last", [P, 1], I32)
        mask = sb("mask", [P, MT, MP])
        w_att = sb("w_att", [P, 4, D])
        w1 = sb("w1", [P, F0])
        w2 = sb("w2", [P, FT, D])
        ln_b = sb("ln_b", [P, 2, D])
        iota = sb("iota", [P, SLOTS])
        lower = sb("lower", [P, P])
        head_rows = sb("head_rows", [P, H])
        freq = sb("freq", [P, HALF])
        diag = sb("diag", [P, T, P])
        counts = sb("counts", [P, 2, T])
        before = sb("before", [P, T])
        rank = sb("rank", [P, T])
        thr_part = sb("thr_part", [P, 1])
        keep = sb("keep", [P, T])
        onehot = sb("onehot", [P, T, SLOTS])
        onehotT = sb("onehotT", [P, NS, S])
        row_last = sb("row_last", [P, SLOTS])
        mask_cols = sb("mask_cols", [P, MT, SLOTS])
        mask_sel = sb("mask_sel", [P, NS, SLOTS])
        xs = sb("xs", [P, NS, D + 2])
        angle = sb("angle", [P, NS, HALF])
        turns = sb("turns", [P, NS, HALF])
        trig = sb("trig", [P, NS, 2, HALF])
        square = sb("square", [P, 2, NS])
        root = sb("root_sel", [P, 2, NS])
        rms = sb("rms", [P, 2, NS])
        newton = sb("newton_sel", [P, 2, NS])
        hn = sb("hn", [P, NS, D])
        hnT = sb("hnT", [P, SLOTS])
        rope = sb("rope", [P, 2, 2 * H, HALF])
        qk = sb("qk", [P, NS, 2 * H, 2, HALF])
        vs = sb("vs", [P, NS, D])
        kT = sb("kT", [P, SLOTS])
        qT = onehot
        LARGER = [t * S - P * (t * (t - 1) // 2) for t in range(T + 1)]
        prob_room = sb("prob", [P, max(H * NS * SEL, LARGER[T] // 2)])
        prob = prob_room[:, 0:H * NS * SEL].rearrange("p (h s k) -> p h s k", h=H, s=NS)
        larger = prob_room[:, 0:LARGER[T] // 2].bitcast(BF16)
        one_b = sb("one_b", [P, 1], BF16)
        probT = diag[:, :, :].rearrange("p t c -> p (t c)")\
            .rearrange("p (n k q) -> p n k q", k=NS, q=SLOTS)
        RING = T * P // (NS * SLOTS)
        top = sb("top", [P, H, NS])
        total = sb("total", [P, NS, H])
        o = sb("o_sel", [P, NS, D])
        oT = sb("oT", [P, SLOTS])
        x1 = sb("x1_sel", [P, NS, D])
        gate = sb("gate_sel", [P, FT * SLOTS])
        proc = sb("proc", [P, NS, D])

        router_loaded = sem("router_loaded")
        mask_loaded = sem("mask_loaded")
        att_loaded = sem("att_loaded")
        mlp_loaded = sem("mlp_loaded")
        pool_step = sem("pool_step")
        consts_set = sem("consts_set")
        diag_done = sem("diag_done")
        spread = sem("spread")
        compared = sem("compared")
        column_summed = sem("column_summed")
        ranked = sem("ranked")
        thr_ready = sem("thr_ready")
        thr_spread = sem("thr_spread")
        gathered = sem("gathered")
        tail_summed = sem("tail_summed")
        clamped = sem("clamped")
        placed = sem("placed")
        placed_out = sem("placed_out")
        cols_taken = sem("cols_taken")
        cols_out = sem("cols_out")
        mask_taken = sem("mask_taken")
        angle_ready = sem("angle_ready")
        trig_done = sem("trig_done")
        square_ready = sem("square_ready")
        root_done = sem("root_sel_done")
        hn_done = sem("hn_done")
        hn_turned = sem("hn_turned")
        hnT_done = sem("hnT_done")
        qkv_done = sem("qkv_done")
        roped = sem("roped")
        qk_turned = sem("qk_turned")
        qkT_done = sem("qkT_done")
        scored = sem("scored_sel")
        masked = sem("masked_sel")
        exped = sem("exped_sel")
        prob_turned = sem("prob_turned")
        probT_done = sem("probT_done")
        weighted = sem("weighted_sel")
        o_done = sem("o_sel_done")
        o_turned = sem("o_turned")
        oT_done = sem("oT_done")
        mixed = sem("mixed")
        hidden = sem("hidden")
        gated = sem("gated")
        downed = sem("downed")
        proc_done = sem("proc_done")
        scattered = sem("scattered")
        combined = sem("combined")
        step = sem("routed_step")

        bank = sh.bank
        weight = sh.xa[:, :, D]
        mask_dram = a["L0_ffn_attention_mask"][0, 0]
        pos_dram = a["L0_ffn_position_ids"][0]

        block = ctx.enter_context(nc.Block())

        @block.sync
        def _(sp):
            sp.dma_start(router_b[:, :], a["L0_ffn_router_w"].rearrange("d o -> (o d)").partition_broadcast(P))\
                .then_inc(router_loaded, 16)
            sp.dma_start(bias_b[:, :], a["L0_ffn_router_b"].partition_broadcast(P)).then_inc(router_loaded, 16)
            sp.dma_start(pos_own[:, :], pos_dram.rearrange("(t p) -> p t", p=P),
                         allow_slow_non_contiguous=True).then_inc(router_loaded, 16)
            sp.dma_start(pos_last[:, :], pos_dram[MP - 1:MP].partition_broadcast(P)).then_inc(router_loaded, 16)
            sp.dma_start(mask[:, :, :], mask_dram.rearrange("(t p) c -> p t c", p=P)).then_inc(mask_loaded, 16)
            for n, name in enumerate(("wq", "wk", "wv", "wo")):
                sp.dma_start(w_att[:, n, :], a["L0_ffn_" + name]).then_inc(att_loaded, 16)
            sp.dma_start(ln_b[:, 0, :], a["L0_ffn_ln1"].partition_broadcast(P)).then_inc(att_loaded, 16)
            sp.dma_start(ln_b[:, 1, :], a["L0_ffn_ln2"].partition_broadcast(P)).then_inc(att_loaded, 16)
            load_rows(sp, sh, 0, sh.q_rows, sh.k_rows, sh.rows_loaded)
            sp.dma_start(w1[:, :], a["L0_ffn_w1"]).then_inc(mlp_loaded, 16)
            sp.dma_start(w2[:, :, :], a["L0_ffn_w2"].rearrange("(t p) d -> p t d", p=P)).then_inc(mlp_loaded, 16)

        @block.gpsimd
        def _(pool):
            link = Chain(pool, pool_step)
            nc.gpsimd.iota(iota[:, :], pattern=[[1, SLOTS]], base=0, channel_multiplier=0,
                           allow_small_or_imprecise_dtypes=True)
            nc.gpsimd.iota(before[:, :], pattern=[[P, T]], base=0, channel_multiplier=0,
                           allow_small_or_imprecise_dtypes=True)
            nc.gpsimd.memset(one_b[:, :], 1.0)
            for n in range(HALF):
                nc.gpsimd.memset(freq[:, n:n + 1], INV_FREQ[n])
            link(nc.gpsimd.memset(lower[:, :], 1.0))
            link(nc.gpsimd.affine_select(out=lower[:, :], in_=lower[:, :], compare_op=ALU.is_gt, fill=0.0,
                                         base=0, pattern=[[-1, P]], channel_multiplier=1))
            link(nc.gpsimd.memset(head_rows[:, :], 1.0 / math.sqrt(HD0)))
            link(nc.gpsimd.affine_select(out=head_rows[:, :], in_=head_rows[:, :], compare_op=ALU.is_ge, fill=0.0,
                                         base=0, pattern=[[-HD0, H]], channel_multiplier=1))
            nc.gpsimd.affine_select(out=head_rows[:, :], in_=head_rows[:, :], compare_op=ALU.is_ge, fill=0.0,
                                    base=HD0 - 1, pattern=[[HD0, H]], channel_multiplier=-1)\
                .then_inc(consts_set, 1)
            nc.gpsimd.memset(sh.v_cols[:, :, :, HD0 + 1:VW], 0.0)
            nc.gpsimd.memset(sh.v_cols[:, :, :, HD0:HD0 + 1], 1.0)
            nc.gpsimd.tensor_copy(sh.v_cols[:, :, :, 0:HD0],
                                  sh.v0[:, :, 0:GH * HD0].rearrange("p t (h j) -> p t h j", j=HD0))

        @block.vector
        def _(dve):
            link = Chain(dve, step)
            dve.wait_ge(router_loaded, 64)
            for t in range(T):
                last = nc.vector.tensor_tensor_reduce(out=diag[:, t, :], in0=sh.xa[:, t, 0:D], in1=router_b[:, :],
                                                      scale=1.0, scalar=0.0, op0=ALU.mult, op1=ALU.add,
                                                      accum_out=rank[:, t:t + 1])
            link(last)
            link(nc.vector.tensor_scalar(weight, rank[:, :], bias_b[:, 0:1], None, ALU.add))
            nc.vector.tensor_copy(sh.xa[:, 0:MT, D + 1], pos_own[:, :])
            link(nc.vector.tensor_copy(sh.xa[:, MT:T, D + 1], pos_last[:, 0:1].to_broadcast([P, T - MT])))
            for t in range(T):
                nc.vector.tensor_scalar(diag[:, t, :], sh.ident[:, :], sh.xa[:, t, D:D + 1], None, ALU.mult)\
                    .then_inc(diag_done, 1)
            dve.wait_ge(spread, 1)
            dve.wait_ge(consts_set, 1)
            every = sh.psum[:, 0:NC, :].rearrange("p b c -> p (b c)")
            for t in range(T):
                own = sh.xa[:, t, D:D + 1]
                nc.vector.tensor_scalar(larger[:, LARGER[t]:LARGER[t + 1]], every[:, t * P:S], own, None, ALU.is_gt,
                                        ALU.add, accum_out=counts[:, 0, t:t + 1]).then_inc(compared, 1)
            for t in range(T):
                last = nc.vector.scalar_tensor_tensor(out=diag[:, t, :], in0=every[:, t * P:(t + 1) * P],
                                                      scalar=sh.xa[:, t, D:D + 1], in1=lower[:, :],
                                                      op0=ALU.is_equal, op1=ALU.mult,
                                                      accum_out=counts[:, 1, t:t + 1])
            link(last)
            link(nc.vector.tensor_tensor(rank[:, :], counts[:, 0, :], counts[:, 1, :], ALU.add))
            link(nc.vector.tensor_tensor(rank[:, :], rank[:, :], before[:, :], ALU.add))
            dve.wait_ge(column_summed, 1)
            link(nc.vector.tensor_tensor(rank[:, 1:T], rank[:, 1:T], bank[4][:, 1:T], ALU.subtract))
            for t in range(T):
                nc.vector.tensor_scalar(onehot[:, t, :], iota[:, :], rank[:, t:t + 1], None, ALU.is_equal)\
                    .then_inc(ranked, 1)
            nc.vector.scalar_tensor_tensor(out=keep[:, :], in0=rank[:, :], scalar=float(SEL), in1=weight,
                                           op0=ALU.is_equal, op1=ALU.mult, accum_out=thr_part[:, :])\
                .then_inc(thr_ready, 1)
            dve.wait_ge(thr_spread, 1)
            link(nc.vector.tensor_scalar(keep[:, :], weight, bank[7][:, 0:1], None, ALU.is_le))
            dve.wait_ge(tail_summed, 1)
            nc.vector.scalar_tensor_tensor(out=row_last[:, :], in0=bank[6][:, 0:SLOTS], scalar=sh.ident[:, P - 1:P],
                                           in1=onehot[:, MT - 1, :], op0=ALU.mult, op1=ALU.add)\
                .then_inc(clamped, 1)
            dve.wait_ge(gathered, 1)
            link(nc.vector.tensor_copy(xs[:, :, :], sh.psum[:, 4:4 + NS, 0:D + 2]))
            def rms_squares(n, src):
                for s in range(NS):
                    last = nc.vector.tensor_tensor_reduce(out=hn[:, s, :], in0=src[:, s, 0:D], in1=src[:, s, 0:D],
                                                          scale=1.0, scalar=0.0, op0=ALU.mult, op1=ALU.add,
                                                          accum_out=square[:, n, s:s + 1])
                link(last)
                nc.vector.tensor_scalar(square[:, n, :], square[:, n, :], 1.0 / D, RMS_EPS, ALU.mult, ALU.add)\
                    .then_inc(square_ready, 1)

            def rms_scale(n, src, turn_bank):
                dve.wait_ge(root_done, n + 1)
                rsqrt_refine(link, nc, rms[:, n, :], root[:, n, :], square[:, n, :], newton[:, n, :])
                for s in range(NS):
                    nc.vector.scalar_tensor_tensor(out=hn[:, s, :], in0=src[:, s, 0:D], scalar=rms[:, n, s:s + 1],
                                                   in1=ln_b[:, n, :], op0=ALU.mult, op1=ALU.mult)\
                        .then_inc(hn_done, 1)
                dve.wait_ge(hn_turned, n + 1)
                nc.vector.tensor_copy(hnT[:, :], turn_bank[:, 0:SLOTS]).then_inc(hnT_done, 1)

            rms_squares(0, xs)
            for s in range(NS):
                last = nc.vector.tensor_scalar(angle[:, s, :], freq[:, :], xs[:, s, D + 1:D + 2], None, ALU.mult)
            link(last)
            link(nc.vector.tensor_scalar(turns[:, :, :], angle[:, :, :], 1.0 / (2.0 * math.pi), ROUND,
                                         ALU.mult, ALU.add))
            link(nc.vector.tensor_scalar(turns[:, :, :], turns[:, :, :], ROUND, None, ALU.subtract))
            for part in TWO_PI:
                link(nc.vector.scalar_tensor_tensor(out=angle[:, :, :], in0=turns[:, :, :], scalar=-part,
                                                    in1=angle[:, :, :], op0=ALU.mult, op1=ALU.add))
            link(nc.vector.tensor_scalar(trig[:, :, 0, :], angle[:, :, :], math.pi / 2, None, ALU.add))
            link(nc.vector.tensor_scalar(turns[:, :, :], trig[:, :, 0, :], 3.1415925, None, ALU.is_gt))
            link(nc.vector.scalar_tensor_tensor(out=trig[:, :, 1, :], in0=turns[:, :, :], scalar=-2.0 * math.pi,
                                                in1=trig[:, :, 0, :], op0=ALU.mult, op1=ALU.add))
            link(nc.vector.tensor_copy(trig[:, :, 0, :], angle[:, :, :]))
            nc.vector.tensor_scalar(trig[:, :, :, :], trig[:, :, :, :], 3.1415925, -3.1415925, ALU.min, ALU.max)\
                .then_inc(angle_ready, 1)
            dve.wait_ge(att_loaded, 96)
            rms_scale(0, xs, bank[6])
            dve.wait_ge(trig_done, 1)
            for s in range(NS):
                dve.wait_ge(qkv_done, s + 1)
                both = bank[4 + s][:, 0:2 * D].rearrange("p (h two j) -> p h two j", two=2, j=HALF)
                sine = trig[:, s, 0:1, :].to_broadcast([P, 2 * H, HALF])
                cosine = trig[:, s, 1:2, :].to_broadcast([P, 2 * H, HALF])
                for half, op in ((0, ALU.subtract), (1, ALU.add)):
                    nc.vector.tensor_tensor(rope[:, 0, :, :], both[:, :, half, :], cosine, ALU.mult)
                    link(nc.vector.tensor_tensor(rope[:, 1, :, :], both[:, :, 1 - half, :], sine, ALU.mult))
                    link(nc.vector.tensor_tensor(qk[:, s, :, half, :], rope[:, 0, :, :], rope[:, 1, :, :], op))
                nc.vector.tensor_copy(vs[:, s, :], bank[4 + s][:, 2 * D:3 * D]).then_inc(roped, 1)
            dve.wait_ge(qk_turned, 1)
            dve.wait_ge(mask_taken, 1)
            nc.vector.tensor_copy(kT[:, :], bank[6][:, SLOTS:2 * SLOTS])
            for h in range(H):
                nc.vector.tensor_scalar(qT[:, h, :], bank[6][:, 0:SLOTS], head_rows[:, h:h + 1], None, ALU.mult)\
                    .then_inc(qkT_done, 1)
            link(nc.vector.tensor_copy(mask_sel[:, :, :], bank[7].rearrange("p (s k) -> p s k", s=NS)))

            def mask_scores(h):
                dve.wait_ge(scored, h + 1)
                for s in range(NS):
                    last = nc.vector.tensor_tensor_reduce(
                        out=prob[:, h, s, :], in0=bank[h % 2][:, s * SLOTS:s * SLOTS + SEL],
                        in1=mask_sel[:, s, 0:SEL], scale=1.0, scalar=-3.0e38, op0=ALU.add, op1=ALU.max,
                        accum_out=top[:, h, s:s + 1])
                link(last)
                nc.vector.tensor_scalar(top[:, h, :], top[:, h, :], -1.0, None, ALU.mult).then_inc(masked, 1)

            def take_probs(h):
                dve.wait_ge(prob_turned, h + 1)
                if h >= RING:
                    dve.wait_ge(weighted, h - RING + 1)
                nc.vector.tensor_copy(probT[:, h % RING, :, :], bank[2 + h % 2].rearrange("p (k q) -> p k q", k=NS))\
                    .then_inc(probT_done, 1)

            for h in range(H + 2):
                if h < H:
                    mask_scores(h)
                if h >= 2:
                    take_probs(h - 2)
            link(nc.vector.reciprocal(total[:, :, :], total[:, :, :]))
            dve.wait_ge(weighted, H)
            nc.vector.tensor_tensor(o[:, :, :].rearrange("p s (h j) -> p s h j", j=HD0),
                                    bank[4][:, 0:NS * D].rearrange("p (s h j) -> p s h j", s=NS, j=HD0),
                                    total[:, :, :].unsqueeze(3).to_broadcast([P, NS, H, HD0]), ALU.mult)\
                .then_inc(o_done, 1)
            dve.wait_ge(o_turned, 1)
            nc.vector.tensor_copy(oT[:, :], bank[5][:, 0:SLOTS]).then_inc(oT_done, 1)
            dve.wait_ge(mixed, 1)
            link(nc.vector.tensor_tensor(x1[:, :, :], bank[6][:, 0:NS * D].rearrange("p (s d) -> p s d", s=NS),
                                         xs[:, :, 0:D], ALU.add))
            rms_squares(1, x1)
            rms_scale(1, x1, bank[7])
            dve.wait_ge(downed, 1)
            link(nc.vector.tensor_tensor(proc[:, :, :], bank[4][:, 0:NS * D].rearrange("p (s d) -> p s d", s=NS),
                                         x1[:, :, :], ALU.add))
            for s in range(NS):
                nc.vector.tensor_scalar(proc[:, s, :], proc[:, s, :], xs[:, s, D:D + 1], None, ALU.mult)\
                    .then_inc(proc_done, 1)
            for c in range(NC):
                dve.wait_ge(scattered, c + 1)
                for j in range(TC):
                    t = c * TC + j
                    last = nc.vector.scalar_tensor_tensor(out=sh.g[:, t, :], in0=sh.xa[:, t, 0:D],
                                                          scalar=keep[:, t:t + 1], in1=bank[c][:, j * P:(j + 1) * P],
                                                          op0=ALU.mult, op1=ALU.add)
                last.then_inc(combined, 1)

        @block.scalar
        def _(act):
            def take_placed(s):
                for c in range(NC):
                    act.wait_ge(placed, s * NC + c + 1)
                    nc.scalar.copy(onehotT[:, s, c * C:(c + 1) * C], bank[c]).then_inc(placed_out, 1)

            act.wait_ge(square_ready, 1)
            nc.scalar.activation(root[:, 0, :], square[:, 0, :], ACT.Sqrt).then_inc(root_done, 1)
            take_placed(0)
            act.wait_ge(angle_ready, 1)
            nc.scalar.activation(trig[:, :, :, :], trig[:, :, :, :], ACT.Sin).then_inc(trig_done, 1)
            take_placed(1)
            for n in range(2):
                act.wait_ge(cols_taken, n + 1)
                nc.scalar.copy(mask_cols[:, 2 * n:2 * n + 2, :], bank[n].rearrange("p (c s) -> p c s", c=2))\
                    .then_inc(cols_out, 1)
            for h in range(H):
                act.wait_ge(masked, h + 1)
                for s in range(NS):
                    last = nc.scalar.activation(prob[:, h, s, :], prob[:, h, s, :], ACT.Exp, bias=top[:, h, s:s + 1],
                                                accum_out=total[:, s, h:h + 1])
                last.then_inc(exped, 1)
            act.wait_ge(square_ready, 2)
            nc.scalar.activation(root[:, 1, :], square[:, 1, :], ACT.Sqrt).then_inc(root_done, 1)
            act.wait_ge(hidden, 1)
            nc.scalar.activation(gate[:, :], sh.psum[:, 0:2, :].rearrange("p b c -> p (b c)"), ACT.Gelu_apprx_tanh)\
                .then_inc(gated, 1)
            for c in range(NC):
                act.wait_ge(combined, c + 1)
                nc.scalar.activation(sh.g[:, c * TC:(c + 1) * TC, :], sh.g[:, c * TC:(c + 1) * TC, :], ACT.Silu)

        @block.tensor
        def _(pe):
            for t in range(T):
                pe.wait_ge(diag_done, t + 1)
                last = nc.tensor.matmul(bank[t // TC][:, (t % TC) * P:(t % TC + 1) * P], sh.ones[:, :], diag[:, t, :],
                                        start=True, stop=True)
            last.then_inc(spread, 1)
            pe.wait_ge(consts_set, 1)
            for later in range(1, T):
                pe.wait_ge(compared, later)
                for t in range(later):
                    at = LARGER[t] + (later - t) * P
                    last = nc.tensor.matmul(bank[4][:, later:later + 1], larger[:, at:at + P], one_b[:, :],
                                            start=(t == 0), stop=(t == later - 1))
            last.then_inc(column_summed, 1)
            pe.wait_ge(ranked, T)
            for s in range(NS):
                for t in range(T):
                    last = nc.tensor.matmul(bank[4 + s][:, 0:D + 2], onehot[:, t, s * P:(s + 1) * P], sh.xa[:, t, :],
                                            start=(t == 0), stop=(t == T - 1))
            last.then_inc(gathered, 1)
            for t in range(MT, T):
                last = nc.tensor.matmul(bank[6][:, 0:SLOTS], sh.ones[:, :], onehot[:, t, :],
                                        start=(t == MT), stop=(t == T - 1))
            last.then_inc(tail_summed, 1)
            pe.wait_ge(thr_ready, 1)
            nc.tensor.matmul(bank[7][:, 0:1], sh.ones[:, :], thr_part[:, :], start=True, stop=True)\
                .then_inc(thr_spread, 1)
            def place(s):
                for c in range(NC):
                    if s:
                        pe.wait_ge(placed_out, (s - 1) * NC + c + 1)
                    for j in range(TC):
                        t = c * TC + j
                        last = nc.tensor.transpose(bank[c][:, j * P:(j + 1) * P], onehot[:, t, s * P:(s + 1) * P],
                                                   sh.ident[:, :])
                    last.then_inc(placed, 1)

            def turn_hn(n, turn_bank):
                for s in range(NS):
                    pe.wait_ge(hn_done, n * NS + s + 1)
                    last = nc.tensor.transpose(turn_bank[:, s * P:(s + 1) * P], hn[:, s, :], sh.ident[:, :])
                last.then_inc(hn_turned, 1)
                pe.wait_ge(hnT_done, n + 1)

            place(0)
            turn_hn(0, bank[6])
            for s in range(NS):
                nc.tensor.matmul(bank[4 + s][:, 0:3 * D], hnT[:, s * P:(s + 1) * P],
                                 w_att[:, 0:3, :], start=True, stop=True).then_inc(qkv_done, 1)
            place(1)
            pe.wait_ge(mask_loaded, 16)
            pe.wait_ge(clamped, 1)
            pe.wait_ge(placed_out, NS * NC)

            def rows(r):
                return row_last[:, :] if r == MT - 1 else onehot[:, r, :]

            for c in range(MT):
                for r in range(MT):
                    last = nc.tensor.matmul(bank[c // 2][:, (c % 2) * SLOTS:(c % 2 + 1) * SLOTS],
                                            mask[:, r, c * P:(c + 1) * P], rows(r),
                                            start=(r == 0), stop=(r == MT - 1))
                if c % 2:
                    last.then_inc(cols_taken, 1)
            pe.wait_ge(cols_out, 2)
            pe.wait_ge(clamped, 1)
            for s in range(NS):
                for c in range(MT):
                    last = nc.tensor.matmul(bank[7][:, s * SLOTS:(s + 1) * SLOTS], mask_cols[:, c, s * P:(s + 1) * P],
                                            rows(c), start=(c == 0), stop=(c == MT - 1))
            last.then_inc(mask_taken, 1)
            for s in range(NS):
                pe.wait_ge(roped, s + 1)
                for m in range(2):
                    last = nc.tensor.transpose(bank[6][:, m * SLOTS + s * P:m * SLOTS + (s + 1) * P],
                                               qk[:, s, m * H:(m + 1) * H, :, :].rearrange("p h two j -> p (h two j)"),
                                               sh.ident[:, :])
            last.then_inc(qk_turned, 1)

            def score(h):
                pe.wait_ge(qkT_done, h + 1)
                if h >= 2:
                    pe.wait_ge(masked, h - 1)
                for s in range(NS):
                    last = nc.tensor.matmul(bank[h % 2][:, s * SLOTS:s * SLOTS + SEL], qT[:, h, s * P:(s + 1) * P],
                                            kT[:, 0:SEL], start=True, stop=True)
                last.then_inc(scored, 1)

            def turn_probs(h):
                pe.wait_ge(exped, h + 1)
                if h >= 2:
                    pe.wait_ge(probT_done, h - 1)
                for k in range(NS):
                    for s in range(NS):
                        last = nc.tensor.transpose(bank[2 + h % 2][0:SELS[k], k * SLOTS + s * P:k * SLOTS + (s + 1) * P],
                                                   prob[:, h, s, k * P:k * P + SELS[k]], sh.ident[:, :])
                last.then_inc(prob_turned, 1)

            def weigh(h):
                pe.wait_ge(probT_done, h + 1)
                for s in range(NS):
                    for k in range(NS):
                        last = nc.tensor.matmul(bank[4][:, s * D + h * HD0:s * D + (h + 1) * HD0],
                                                probT[0:SELS[k], h % RING, k, s * P:(s + 1) * P],
                                                vs[0:SELS[k], k, h * HD0:(h + 1) * HD0],
                                                start=(k == 0), stop=(k == NS - 1))
                last.then_inc(weighted, 1)

            for h in range(H + 4):
                if h < H:
                    score(h)
                if 2 <= h < H + 2:
                    turn_probs(h - 2)
                if h >= 4:
                    weigh(h - 4)
            pe.wait_ge(o_done, 1)
            for s in range(NS):
                last = nc.tensor.transpose(bank[5][:, s * P:(s + 1) * P], o[:, s, :], sh.ident[:, :])
            last.then_inc(o_turned, 1)
            pe.wait_ge(oT_done, 1)
            for s in range(NS):
                last = nc.tensor.matmul(bank[6][:, s * D:(s + 1) * D], oT[:, s * P:(s + 1) * P], w_att[:, 3, :],
                                        start=True, stop=True)
            last.then_inc(mixed, 1)
            turn_hn(1, bank[7])
            pe.wait_ge(mlp_loaded, 32)
            for f in range(FT):
                last = nc.tensor.matmul(bank[f // 2][:, (f % 2) * SLOTS:(f % 2 + 1) * SLOTS], w1[:, f * P:(f + 1) * P],
                                        hnT[:, :], start=True, stop=True)
            last.then_inc(hidden, 1)
            pe.wait_ge(gated, 1)
            for s in range(NS):
                for f in range(FT):
                    last = nc.tensor.matmul(bank[4][:, s * D:(s + 1) * D],
                                            gate[:, f * SLOTS + s * P:f * SLOTS + (s + 1) * P], w2[:, f, :],
                                            start=(f == 0), stop=(f == FT - 1))
            last.then_inc(downed, 1)
            pe.wait_ge(proc_done, NS)
            for t in range(T):
                for s in range(NS):
                    last = nc.tensor.matmul(bank[t // TC][:, (t % TC) * P:(t % TC + 1) * P],
                                            onehotT[0:SELS[s], s, t * P:(t + 1) * P], proc[0:SELS[s], s, :],
                                            start=(s == 0), stop=(s == NS - 1))
                if t % TC == TC - 1:
                    last.then_inc(scattered, 1)


def join0(nc, a, sh):
    with ExitStack() as ctx:
        def sb(name, shape, dt=F32):
            return ctx.enter_context(nc.sbuf_tensor(name, shape, dt))

        def sem(name):
            return ctx.enter_context(nc.semaphore(name))

        w_out = sb("w_out", [P, D])
        rows = sb("rows", [P, 3, D])
        oT = sb("o0T", [P, S])
        y = sb("y", [P, T, D])
        stats = sb("stats_j", [P, T, 6])
        moments = sb("moments_j", [P, T, 2])
        var_eps = sb("var_eps_j", [P, 2, T])
        root = sb("root_j", [P, 2, T])
        rstd = sb("rstd_j", [P, 2, T])
        newton = sb("newton_j", [P, T])

        w_loaded = sem("w_out_loaded")
        turned = sem("o0_turned")
        oT_done = sem("o0T_done")
        projected = sem("o0_projected")
        var_done = sem("var_done_j")
        root_done = sem("root_done_j")
        normed = sem("normed_j")
        xn_turned = sem("xn_turned_j")
        xnT_done = sem("xnT_done_j")
        step = sem("join_step")
        bank = sh.bank

        block = ctx.enter_context(nc.Block())

        @block.sync
        def _(sp):
            sp.dma_start(w_out[:, :], a["L0_attn_w_out"]).then_inc(w_loaded, 16)
            for n, name in enumerate(("b_out", "gamma", "beta")):
                sp.dma_start(rows[:, n, :], a["L0_attn_" + name].partition_broadcast(P)).then_inc(w_loaded, 16)

        @block.tensor
        def _(pe):
            for c in range(NC):
                for j in range(TC):
                    for group in range(G):
                        rows_of = slice(group * GH * HD0, (group + 1) * GH * HD0)
                        last = nc.tensor.matmul(bank[c][rows_of, j * P:(j + 1) * P],
                                                sh.o0[:, 1 + group * NC + c, j, :], sh.ident[:, :],
                                                start=True, stop=True)
                last.then_inc(turned, 1)
            pe.wait_ge(w_loaded, 64)
            for c in range(NC):
                pe.wait_ge(oT_done, c + 1)
                for j in range(TC):
                    t = c * TC + j
                    last = nc.tensor.matmul(bank[4 + c][:, j * P:(j + 1) * P], oT[:, t * P:(t + 1) * P], w_out[:, :],
                                            start=True, stop=True)
                last.then_inc(projected, 1)
            for c in range(NC):
                pe.wait_ge(normed, (c + 1) * TC)
                for j in range(TC):
                    last = nc.tensor.transpose(bank[c][:, j * P:(j + 1) * P], sh.xa[:, c * TC + j, 0:D], sh.ident[:, :])
                last.then_inc(xn_turned, 1)

        @block.scalar
        def _(act):
            for c in range(NC):
                act.wait_ge(turned, c + 1)
                nc.scalar.copy(oT[:, c * C:(c + 1) * C], bank[c]).then_inc(oT_done, 1)
            for n in range(2):
                act.wait_ge(var_done, n + 1)
                nc.scalar.activation(root[:, n, :], var_eps[:, n, :], ACT.Sqrt).then_inc(root_done, 1)
            for c in range(NC):
                act.wait_ge(xn_turned, c + 1)
                nc.scalar.copy(sh.xnT[:, c * C:(c + 1) * C], bank[c]).then_inc(xnT_done, 1)

        @block.vector
        def _(dve):
            link = Chain(dve, step)

            def moments_of(n, src):
                for t in range(T):
                    last = nc.vector.bn_stats(stats[:, t, :], src[:, t, :])
                link(last)
                for t in range(T):
                    last = nc.vector.bn_aggr(moments[:, t, :], stats[:, t, :])
                link(last)
                nc.vector.tensor_scalar(var_eps[:, n, :], moments[:, :, 1], LN_EPS, None, ALU.add)\
                    .then_inc(var_done, 1)
                dve.wait_ge(root_done, n + 1)
                rsqrt_refine(link, nc, rstd[:, n, :], root[:, n, :], var_eps[:, n, :], newton[:, :])

            def row(n):
                return rows[:, n:n + 1, :].to_broadcast([P, T, D])

            dve.wait_ge(w_loaded, 64)
            for c in range(NC):
                at = slice(c * TC, (c + 1) * TC)
                dve.wait_ge(projected, c + 1)
                last = nc.vector.tensor_tensor(y[:, at, :], bank[4 + c].rearrange("p (t d) -> p t d", d=D),
                                               sh.xa[:, at, 0:D], ALU.add)
            link(last)
            link(nc.vector.tensor_tensor(y[:, :, :], y[:, :, :], row(0), ALU.add))
            moments_of(0, y)
            for t in range(T):
                last = nc.vector.tensor_scalar(y[:, t, :], y[:, t, :], moments[:, t, 0:1], rstd[:, 0, t:t + 1],
                                               ALU.subtract, ALU.mult)
            link(last)
            link(nc.vector.tensor_tensor(y[:, :, :], y[:, :, :], row(1), ALU.mult))
            link(nc.vector.tensor_tensor(y[:, :, :], y[:, :, :], row(2), ALU.add))
            link(nc.vector.tensor_tensor(y[:, :, :], y[:, :, :], sh.g[:, :, :], ALU.mult))
            link(nc.vector.tensor_tensor(sh.x[:, :, :], sh.x[:, :, :], y[:, :, :], ALU.add))
            moments_of(1, sh.x)
            for t in range(T):
                nc.vector.tensor_scalar(sh.xa[:, t, 0:D], sh.x[:, t, :], moments[:, t, 0:1], rstd[:, 1, t:t + 1],
                                        ALU.subtract, ALU.mult).then_inc(normed, 1)


def gated1(nc, a, sh):
    with ExitStack() as ctx:
        def sb(name, shape, dt=F32):
            return ctx.enter_context(nc.sbuf_tensor(name, shape, dt))

        def sem(name):
            return ctx.enter_context(nc.semaphore(name))

        w_int = sb("w_int", [P, 3, F1], I32)
        w_real = sb("w_real", [P, 3, F1])
        wT = sb("wT", [P, 3, F1])
        act_gate = sb("act_gate", [P, 2, C])
        inner = sb("inner", [P, F1T, S])

        w_loaded = sem("w1_loaded")
        w_scaled = sem("w1_scaled")
        w_turned = sem("w1_turned")
        wT_done = sem("w1T_done")
        gate_done = sem("gate1_done")
        gate_act = sem("gate1_act")
        inner_done = sem("inner1_done")
        down_done = sem("down1_done")
        g_done = sem("g1_done")
        bank = sh.bank

        block = ctx.enter_context(nc.Block())

        @block.sync
        def _(sp):
            for n, name in enumerate(("w_gate", "w_up")):
                sp.dma_start(w_int[:, n, :].rearrange("p (t d) -> p t d", d=D),
                             a["L1_ffn_" + name].rearrange("(t p) d -> p t d", p=P)).then_inc(w_loaded, 16)
            sp.dma_start(w_int[:, 2, :], a["L1_ffn_w_down"]).then_inc(w_loaded, 16)

        @block.tensor
        def _(pe):
            for n in range(3):
                pe.wait_ge(w_scaled, n + 1)
                for f in range(F1T):
                    last = nc.tensor.transpose(bank[n][:, f * P:(f + 1) * P], w_real[:, n, f * P:(f + 1) * P],
                                               sh.ident[:, :])
                last.then_inc(w_turned, 1)
            pe.wait_ge(wT_done, 3)
            for f in range(F1T):
                for c in range(NC):
                    n = f * NC + c
                    if n >= 2:
                        pe.wait_ge(inner_done, n - 1)
                    for m in range(2):
                        last = nc.tensor.matmul(bank[2 * (n % 2) + m], wT[:, m, f * P:(f + 1) * P],
                                                sh.xnT[:, c * C:(c + 1) * C], start=True, stop=True)
                    last.then_inc(gate_done, 1)
            pe.wait_ge(inner_done, F1T * NC)
            for c in range(NC):
                for j in range(TC):
                    t = c * TC + j
                    for f in range(F1T):
                        last = nc.tensor.matmul(bank[4 + c][:, j * P:(j + 1) * P], inner[:, f, t * P:(t + 1) * P],
                                                wT[:, 2, f * P:(f + 1) * P], start=(f == 0), stop=(f == F1T - 1))
                last.then_inc(down_done, 1)

        @block.scalar
        def _(act):
            for n in range(3):
                act.wait_ge(w_turned, n + 1)
                nc.scalar.copy(wT[:, n, :], bank[n][:, 0:F1]).then_inc(wT_done, 1)
            for n in range(F1T * NC):
                act.wait_ge(gate_done, n + 1)
                if n >= 2:
                    act.wait_ge(inner_done, n - 1)
                nc.scalar.activation(act_gate[:, n % 2, :], bank[2 * (n % 2)], ACT.Silu).then_inc(gate_act, 1)
            for c in range(NC):
                act.wait_ge(down_done, c + 1)
                nc.scalar.activation(sh.g[:, c * TC:(c + 1) * TC, :], bank[4 + c].rearrange("p (t d) -> p t d", d=D),
                                     ACT.Silu).then_inc(g_done, 1)

        @block.vector
        def _(dve):
            dve.wait_ge(w_loaded, 48)
            for n in range(3):
                nc.vector.tensor_scalar(w_real[:, n, :], w_int[:, n, :], Q_SCALE, None, ALU.mult).then_inc(w_scaled, 1)
            for n in range(F1T * NC):
                f, c = n // NC, n % NC
                dve.wait_ge(gate_act, n + 1)
                nc.vector.tensor_tensor(inner[:, f, c * C:(c + 1) * C], act_gate[:, n % 2, :], bank[2 * (n % 2) + 1],
                                        ALU.mult).then_inc(inner_done, 1)


def one(ap, n, axis):
    if isinstance(n, int):
        return ap[n] if axis == 0 else ap[:, n]
    if axis == 0:
        return ap[bass.ds(n, 1)].rearrange("o m d -> (o m) d")
    if len(ap.shape) == 3:
        return ap[:, bass.ds(n, 1), :].rearrange("p o m -> p (o m)")
    return ap[:, bass.ds(n, 1), :, :].rearrange("p o t d -> p (o t) d")


def column(bias, m, h, part):
    return bias[part, m, h:h + 1] if isinstance(h, int) else bias[part, m, bass.ds(h, 1)]


def attention1(nc, a, sh, out):
    with ExitStack() as ctx:
        def sb(name, shape, dt=F32):
            return ctx.enter_context(nc.sbuf_tensor(name, shape, dt))

        def sem(name):
            return ctx.enter_context(nc.semaphore(name))

        W = HD1
        MR = W + TC
        TOP, LOW = slice(0, W), slice(W, 2 * W)
        PR = 4
        LEAD = 2
        SCALE = 1.0 / math.sqrt(HD1)
        PAIRS = [(qc, j) for qc in range(NC) for j in range(2 * qc + 2)]
        NPAIR = len(PAIRS)
        BODY = 2

        maxima = [[("maximum", (i, c)) for i in range(qc * TC, (qc + 1) * TC) for c in range(qc + 1)]
                  for qc in range(NC)]
        UNIT = [("project", qc) for qc in range(NC)] + maxima[0]
        for qc in range(1, NC):
            UNIT += maxima[qc][:6] + [("turn", qc - 1)] + maxima[qc][6:]
        UNIT += [("turn", NC - 1)]
        UNITS = len(UNIT)
        PROJECT = [UNIT.index(("project", c)) for c in range(NC)]
        TURN = [UNIT.index(("turn", c)) for c in range(NC)]

        GAPS = 5
        END = NPAIR * GAPS - 1
        HOLD = {"project": 5, "maximum": 2, "turn": 3}
        READY = {"project": 11, "maximum": 5}
        PROJECT_SLOT = {0: 1, 1: 5, 2: 8, 3: 11}
        CHUNK_END = [(qc + 1) * (qc + 2) - 1 for qc in range(NC)]
        MIX_STEP = [min(n + 1, NPAIR - 1) for n in CHUNK_END]
        SUM_STEP = [min(n + 2, NPAIR - 1) for n in CHUNK_END]
        ADD_STEP = [n + 1 for n in SUM_STEP[:-1]]
        near_sums = [n * GAPS + gap for n in SUM_STEP for gap in range(GAPS - 2, GAPS + 1)]
        slot_units = [[] for _ in range(END + 1)]
        late_units = [[] for _ in range(END + 1)]
        BANK, free, ready, at_slot = [], [2, 0], {}, 0
        for u, (kind, what) in enumerate(UNIT):
            if kind == "project":
                earliest = PROJECT_SLOT[what]
            else:
                first = PROJECT_SLOT[0] + READY["project"]
                spread = first + (u - NC) * (END - first) // (UNITS - 1 - NC)
                source = ("maximum", what) if kind == "turn" else ("project", what[0] // TC)
                earliest = max(spread, at_slot + 1, ready[source])
            slots = [max(earliest, free[b]) for b in range(2)]
            while slots[0] in near_sums:
                slots[0] += 1
            b = 0 if slots[0] <= slots[1] and free[0] <= free[1] or slots[0] < slots[1] else 1
            at_slot = min(slots[b], END)
            BANK.append(b)
            slot_units[at_slot].append(u)
            late_units[min(at_slot + (2 if kind == "project" else 0), END)].append(u)
            free[b] = at_slot + HOLD[kind]
            if kind == "project":
                ready[kind, what] = at_slot + READY[kind]
            elif kind == "maximum":
                ready[kind, what[0] // TC] = at_slot + READY[kind]
        FREED = [BANK[:u + 1].count(BANK[u]) for u in range(UNITS)]
        BANK_FREES = [BANK.count(b) for b in range(2)]

        wkq = [sb(f"wkq{n}", [P, 2 * W]) for n in range(2)]
        wo = sb("wo", [P, H, D])
        bias = sb("bias", [P, H])
        row_o = sb("row_o", [P, D])
        q_hi = [sb(f"q_hi{n}", [P, S], F32R) for n in range(2)]
        k_both = [sb(f"k_both{n}", [P, S], F32R) for n in range(2)]
        q_lo = [sb(f"q_lo{n}", [P, S], F32R) for n in range(2)]
        k_hi = [sb(f"k_hi{n}", [P, S], F32R) for n in range(2)]
        causal = sb("causal", [P, P], BF16)
        never = sb("never", [P, P], BF16)
        ident_b = sb("ident_b", [P, P], BF16)
        v_all = sb("v_all", [P, H, T, W])
        v_head = [sb(f"v_head{n}", [P, T, W]) for n in range(2)]
        prob = sb("prob1", [P, PR, 2, C])
        acc = sb("acc", [P, 2, C])
        z = sb("z", [P, C])
        part_max = sb("part_max", [P, T, NC])
        neg_max = sb("neg_max", [P, T])
        own_tile = sb("own_tile", [TC, TC, P])
        inv = sb("inv", [P, TC])
        attn = sh.xa[:, :, 0:D]
        rows = prob[:, 0, :, :].rearrange("p m c -> p (m c)")
        bias_rows = acc[0:H, 0, 0:2 * W]
        wv = v_head[0][:, :, :].rearrange("p t d -> p (t d)")

        bias_loaded = sem("bias_loaded")
        wv_loaded = sem("wv_loaded")
        rows_loaded1 = sem("rows_loaded1")
        wo_loaded = sem("wo_loaded")
        qk_loaded = [sem(f"qk_loaded{n}") for n in range(2)]
        v_loaded = [sem(f"v_loaded{n}") for n in range(2)]
        consts_set = sem("consts1_set")
        pool_step = sem("pool1_step")
        bias_turned = sem("bias_turned")
        bias_done = sem("bias_done")
        v_projected = sem("v1_projected")
        v_done = sem("v1_done")
        prep_filled = sem("prep_filled")
        prep_freed = [sem(f"prep_freed{b}") for b in range(2)]
        act_split = sem("act_split")
        doubled = [sem(f"doubled{c}") for c in range(NC)]
        max_done = sem("max_done")
        part_step = sem("part_step")
        st_filled = sem("st_filled")
        exp_done = sem("exp_done")
        weighted = sem("weighted1")
        summed = sem("summed")
        z_copied = sem("z_copied")
        mixed = sem("mixed1")
        inv_done = sem("inv_done")
        sum_done = sem("sum_done")
        added = sem("added")
        result_step = sem("result_step")
        act_passed = sem("act_passed")
        result_done = sem("result_done")
        stored = sem("stored")

        bank = sh.bank
        st_slot = [sh.psum[:, 2 * n:2 * n + 2, :] for n in range(2)]
        v_bank = bank[0:4]
        prep_bank = bank[4:6]
        sum_bank = prep_bank[0]
        out_bank = bank[6:8]

        block = ctx.enter_context(nc.Block())


        def first_column(qc, j, m=0):
            return max(0, (2 * j + m) * P - qc * C)

        def wait_freed(engine, h, u):
            engine.wait_ge(prep_freed[BANK[u]], h * BANK_FREES[BANK[u]] + FREED[u])

        def heads(engine, body):
            with engine.Fori(0, H // BODY - 1) as n:
                for p in range(BODY):
                    body(engine.snap(n * BODY + p), p, True)
            for p in range(BODY):
                body(H - BODY + p, p, p < BODY - 1)

        def ahead(h, p, n, more):
            if n + LEAD < NPAIR:
                return [(h, p, n + LEAD)]
            return [(h + 1, 1 - p, n + LEAD - NPAIR)] if more else []

        @block.sync
        def _(sp):
            for m, name in enumerate(("b_K", "b_Q")):
                sp.dma_start(bias_rows[:, m * W:(m + 1) * W], a["L1_attn_" + name]).then_inc(bias_loaded, 16)
            sp.dma_start(wv.rearrange("m (h d) -> m h d", d=W), a["L1_attn_W_V"].rearrange("h m d -> m h d"))\
                .then_inc(wv_loaded, 16)

            def load_qk(h, p):
                for n, name in enumerate(("W_K", "W_Q")):
                    sp.dma_start(wkq[p][:, n * W:(n + 1) * W], one(a["L1_attn_" + name], h, 0))\
                        .then_inc(qk_loaded[p], 16)

            def load_v(h, p):
                sp.dma_start(v_head[p][:, :, :], one(v_all, h, 1)).then_inc(v_loaded[p], 16)

            def double_high(h, p, c):
                at = slice(c * C, (c + 1) * C)
                sp.wait_ge(act_split, (h * NC + c) * 2 + 1)
                sp.dma_start(k_hi[p][TOP, at].bitcast(F32), k_both[p][TOP, at].bitcast(F32)).then_inc(doubled[c], 16)
                sp.wait_ge(act_split, (h * NC + c) * 2 + 2)
                sp.dma_start(q_hi[p][TOP, at].bitcast(F32), q_hi[p][LOW, at].bitcast(F32)).then_inc(doubled[c], 16)

            load_qk(0, 0)
            sp.dma_start(rows[:, :], a["L1_attn_b_V"].rearrange("h d -> (h d)").partition_broadcast(P))\
                .then_inc(rows_loaded1, 16)
            sp.dma_start(row_o[:, :], a["L1_attn_b_O"].partition_broadcast(P)).then_inc(rows_loaded1, 16)
            load_qk(1, 1)
            for n in range(2):
                sp.dma_start(wo[n * W:(n + 1) * W, :, :], a["L1_attn_W_O"].rearrange("h d m -> d h m"))\
                    .then_inc(wo_loaded, 16)
            for c in range(NC):
                double_high(0, 0, c)
            sp.wait_ge(v_done, 2 * T)
            for h in range(2):
                load_v(h, h)
            with sp.Fori(0, H // BODY - 1) as n:
                for p in range(BODY):
                    h = sp.snap(n * BODY + p)
                    sp.wait_ge(prep_filled, h * UNITS + (PROJECT[-1] + 1))
                    load_qk(h + 2, p)
                    for c in range(NC):
                        double_high(h + 1, 1 - p, c)
                    sp.wait_ge(weighted, (h + 1) * NPAIR + PR)
                    load_v(h + 2, p)
            for c in range(NC):
                double_high(H - 1, (H - 1) % 2, c)
            for c in range(NC):
                sp.wait_ge(result_done, c + 1)
                sp.dma_start(out[0].rearrange("(t p) d -> p t d", p=P)[:, c * TC:(c + 1) * TC, :],
                             attn[:, c * TC:(c + 1) * TC, :]).then_inc(stored, 16)
            sp.wait_ge(stored, 16 * NC)

        @block.gpsimd
        def _(pool):
            pool.sem_inc(exp_done, 2)
            pool.sem_inc(weighted, PR)
            pool.sem_inc(summed, PR)
            pool.sem_inc(sum_done, 2)
            pool.sem_inc(mixed, 1)
            pool.sem_inc(inv_done, 1)
            pool.sem_inc(added, 2)
            link = Chain(pool, pool_step)
            link(nc.gpsimd.memset(causal[:, :], 0.0))
            link(nc.gpsimd.affine_select(out=causal[:, :], in_=causal[:, :], compare_op=ALU.is_ge, fill=NEG,
                                         base=0, pattern=[[-1, P]], channel_multiplier=1))
            link(nc.gpsimd.memset(never[:, :], NEG))
            link(nc.gpsimd.tensor_copy(ident_b[:, :], sh.ident[:, :]))
            for n in range(2):
                nc.gpsimd.memset(k_hi[n][W:MR, :].bitcast(F32), 1.0)
            link(nc.gpsimd.memset(own_tile[:, :, :], 0.0))
            nc.gpsimd.affine_select(out=own_tile[:, :, :], in_=own_tile[:, :, :], compare_op=ALU.not_equal, fill=1.0,
                                    base=0, pattern=[[-1, TC], [0, P]], channel_multiplier=1).then_inc(consts_set, 1)

            def body(h, p, more):
                for n, (qc, j) in enumerate(PAIRS):
                    pool.wait_ge(exp_done, h * NPAIR + (n + 3))
                    pair = prob[:, n % PR, :, :]
                    sums = acc[:, qc % 2, :]
                    if j == 0:
                        pool.wait_ge(sum_done, h * NC + (qc + 1))
                        nc.gpsimd.tensor_tensor(sums, pair[:, 0, :], pair[:, 1, :], ALU.add).then_inc(summed, 1)
                    else:
                        q0, q1 = first_column(qc, j), first_column(qc, j, 1)
                        pool.wait_ge(summed, h * NPAIR + (n + PR))
                        nc.gpsimd.tensor_tensor(sums[:, q0:C], sums[:, q0:C], pair[:, 0, q0:C], ALU.add)\
                            .then_inc(part_step, 1)
                        pool.wait_ge(part_step, h * (NPAIR - NC) + (n - qc))
                        nc.gpsimd.tensor_tensor(sums[:, q1:C], sums[:, q1:C], pair[:, 1, q1:C], ALU.add)\
                            .then_inc(summed, 1)

            heads(pool, body)

        @block.tensor
        def _(pe):
            pe.wait_ge(bias_loaded, 32)
            nc.tensor.transpose(out_bank[0][:, 0:H], bias_rows, sh.ident[0:H, 0:H]).then_inc(bias_turned, 1)

            def project_v(u):
                t, n = u // 2, u % 2
                if u >= len(v_bank):
                    pe.wait_ge(v_done, u - len(v_bank) + 1)
                nc.tensor.matmul(v_bank[u % len(v_bank)], sh.xnT[:, t * P:(t + 1) * P], wv[:, n * C:(n + 1) * C],
                                 start=True, stop=True).then_inc(v_projected, 1)

            def prepare_unit(h, p, u, sums=None):
                kind, what = UNIT[u]
                to = prep_bank[BANK[u]]
                before = FREED[u] - 1
                if before or not (isinstance(h, int) and h == 0):
                    pe.wait_ge(prep_freed[BANK[u]], h * BANK_FREES[BANK[u]] + before)
                if sums is not None:
                    pe.wait_ge(inv_done, sums)
                if kind == "project":
                    last = nc.tensor.matmul(to, wkq[p][:, :], sh.xnT[:, what * C:(what + 1) * C],
                                            start=True, stop=True)
                elif kind == "maximum":
                    i, c = what
                    if c == 0 and i % TC == 0:
                        wait_freed(pe, h, PROJECT[i // TC])
                        pe.wait_ge(doubled[i // TC], (h + 1) * 32)
                    n = min(C, (i + 1) * P - c * C)
                    diagonal = c == i // TC
                    last = nc.tensor.matmul(to[:, 0:n], q_hi[p][:, i * P:(i + 1) * P], k_both[p][:, c * C:c * C + n],
                                            start=True, stop=not diagonal)
                    if diagonal:
                        last = nc.tensor.matmul(to[:, n - P:n], ident_b[:, :], causal[:, :], start=False, stop=True)
                else:
                    pe.wait_ge(max_done, h * NC + (what + 1))
                    last = nc.tensor.transpose(to[0:TC, 0:P], neg_max[:, what * TC:(what + 1) * TC], sh.ident[:, :])
                last.then_inc(prep_filled, 1)

            def score_half(h, p, n, m):
                qc, j = PAIRS[n]
                if m == 0:
                    pe.wait_ge(exp_done, h * NPAIR + (n + 1))
                    if j == 0:
                        wait_freed(pe, h, TURN[qc])
                q0 = first_column(qc, j, m)
                at = slice(qc * C + q0, (qc + 1) * C)
                kt = slice((2 * j + m) * P, (2 * j + m + 1) * P)
                bank_m = st_slot[n % 2][:, m, :]
                diagonal = j >= 2 * qc
                if diagonal and m == 1:
                    nc.tensor.matmul(bank_m[:, q0 - P:q0], ident_b[:, :], never[:, :], start=True, stop=True)
                nc.tensor.matmul(bank_m[:, q0:C], k_both[p][:, kt], q_hi[p][:, at], start=True, stop=False)
                last = nc.tensor.matmul(bank_m[:, q0:C], k_hi[p][0:MR, kt], q_lo[p][0:MR, at],
                                        start=False, stop=not diagonal)
                if diagonal:
                    last = nc.tensor.matmul(bank_m[:, q0:q0 + P], causal[:, :], ident_b[:, :], start=False, stop=True)
                if m == 1:
                    last.then_inc(st_filled, 1)

            def weigh(h, p, n):
                qc, j = PAIRS[n]
                pe.wait_ge(exp_done, h * NPAIR + (n + 3))
                if j == 0:
                    pe.wait_ge(added, h * NC + (qc + 1))
                for m in range(2):
                    q0 = 0 if j == 0 else first_column(qc, j, m)
                    last = nc.tensor.matmul(out_bank[qc % 2][m * W:(m + 1) * W, q0:C], v_head[p][:, 2 * j + m, :],
                                            prob[:, n % PR, m, q0:C], start=(j == 0), stop=(j == 2 * qc + 1))
                last.then_inc(weighted, 1)

            def mix(h, qc):
                pe.wait_ge(z_copied, h * NC + (qc + 1))
                for j in range(TC):
                    last = nc.tensor.matmul(out_bank[qc % 2][:, j * P:(j + 1) * P], z[:, j * P:(j + 1) * P], one(wo, h, 1),
                                            start=True, stop=True)
                last.then_inc(mixed, 1)

            def take_sums(h, qc, before):
                pe.wait_ge(prep_freed[0], before)
                pe.wait_ge(inv_done, h * NC + (qc + 1))
                pe.wait_ge(summed, h * NPAIR + (CHUNK_END[qc] + 1 + PR))
                for j in range(TC):
                    last = nc.tensor.matmul(sum_bank[:, j:j + 1], acc[:, qc % 2, j * P:(j + 1) * P], sh.ones[:, 0:1],
                                            start=True, stop=True)
                last.then_inc(sum_done, 1)

            pe.wait_ge(wv_loaded, 16)
            pe.wait_ge(rows_loaded1, 32)
            pe.wait_ge(consts_set, 1)
            pe.wait_ge(bias_done, 1)
            pe.wait_ge(qk_loaded[0], 32)
            for s in range(NPAIR * GAPS):
                if s % 2 == 0 and s < 4 * T:
                    project_v(s // 2)
                for u in slot_units[s]:
                    prepare_unit(0, 0, u)
            pe.wait_ge(v_done, 2 * T)
            pe.wait_ge(wo_loaded, 32)
            for n in range(LEAD):
                for m in range(2):
                    score_half(0, 0, n, m)

            def body(h, p, more):
                pe.wait_ge(v_loaded[p], (h + (2 - p)) * 8)
                if more:
                    pe.wait_ge(qk_loaded[1 - p], (h + (p + 2)) * 16)
                freed = 0
                sums = h * NC + 1
                for n, (qc, j) in enumerate(PAIRS):
                    for gap in range(GAPS):
                        if gap == 1:
                            weigh(h, p, n)
                        if gap in (2, 3):
                            for args in ahead(h, p, n, more):
                                score_half(*args, gap - 2)
                        if gap == GAPS - 1 and n in MIX_STEP:
                            mix(h, MIX_STEP.index(n))
                        if gap == GAPS - 1 and n in SUM_STEP:
                            take_sums(h, SUM_STEP.index(n), (h + 1) * BANK_FREES[0] + freed)
                            sums = h * NC + (SUM_STEP.index(n) + 2)
                        if more:
                            for u in slot_units[n * GAPS + gap]:
                                if BANK[u] == 0:
                                    prepare_unit(h + 1, 1 - p, u, sums)
                                    freed, sums = FREED[u], None
                                else:
                                    prepare_unit(h + 1, 1 - p, u)

            heads(pe, body)

        @block.scalar
        def _(act):
            act.wait_ge(bias_turned, 1)
            nc.scalar.copy(bias[:, :], out_bank[0][:, 0:H]).then_inc(bias_done, 1)
            act.wait_ge(bias_done, 1)

            def prepare_unit(h, p, u):
                kind, what = UNIT[u]
                src = prep_bank[BANK[u]]
                if kind == "project":
                    at = slice(what * C, (what + 1) * C)
                    act.wait_ge(prep_filled, h * UNITS + (u + 1))
                    act.sem_inc(act_passed, 1)
                    bias_k = bias[TOP, h:h + 1] if isinstance(h, int) else bias[TOP, bass.ds(h, 1)]
                    bias_q = bias[LOW, h:h + 1] if isinstance(h, int) else bias[LOW, bass.ds(h, 1)]
                    nc.scalar.activation(k_both[p][TOP, at], src[TOP, :], ACT.Identity, bias=bias_k)\
                        .then_inc(act_split, 1)
                    nc.scalar.activation(q_hi[p][LOW, at], src[LOW, :], ACT.Identity, bias=bias_q)\
                        .then_inc(act_split, 1)

            def copy_out(h, qc):
                turn = h * NC + qc
                act.wait_ge(weighted, h * NPAIR + (CHUNK_END[qc] + 1 + PR))
                act.wait_ge(mixed, turn + 1)
                nc.scalar.copy(z[:, :], out_bank[qc % 2]).then_inc(z_copied, 1)

            def exponentials(h, n):
                qc, j = PAIRS[n]
                q0 = first_column(qc, j)
                act.wait_ge(st_filled, h * NPAIR + (n + 1))
                act.wait_ge(weighted, h * NPAIR + (n + 1))
                act.wait_ge(summed, h * NPAIR + (n + 1))
                nc.scalar.activation(prob[:, n % PR, :, q0:C], st_slot[n % 2][:, :, q0:C], ACT.Exp, scale=SCALE)\
                    .then_inc(exp_done, 1)

            for s in range(NPAIR * GAPS):
                for u in slot_units[s]:
                    prepare_unit(0, 0, u)
            for n in range(LEAD):
                exponentials(0, n)

            def body(h, p, more):
                for n in range(NPAIR):
                    for gap in range(GAPS):
                        if gap == 3:
                            if n in CHUNK_END:
                                copy_out(h, CHUNK_END.index(n))
                            for head, _, pair in ahead(h, p, n, more):
                                exponentials(head, pair)
                        if more:
                            for u in slot_units[n * GAPS + gap]:
                                prepare_unit(h + 1, 1 - p, u)

            heads(act, body)

        @block.vector
        def _(dve):
            link = Chain(dve, result_step)
            dve.wait_ge(rows_loaded1, 32)
            link(nc.vector.tensor_copy(attn[:, :, :], row_o[:, :].unsqueeze(1).to_broadcast([P, T, D])))
            dve.wait_ge(bias_done, 1)
            dve.wait_ge(consts_set, 1)

            def bias_v(u):
                t, n = u // 2, u % 2
                half = slice(n * H // 2, (n + 1) * H // 2)
                dve.wait_ge(v_projected, u + 1)
                nc.vector.tensor_tensor(v_all[:, half, t, :], v_bank[u % len(v_bank)].rearrange("p (h d) -> p h d", d=W),
                                        rows[:, n * C:(n + 1) * C].rearrange("p (h d) -> p h d", d=W), ALU.add)\
                    .then_inc(v_done, 1)

            def prepare_unit(h, p, u):
                kind, what = UNIT[u]
                src = prep_bank[BANK[u]]
                if kind == "project":
                    at = slice(what * C, (what + 1) * C)
                    bias_k = bias[TOP, h:h + 1] if isinstance(h, int) else bias[TOP, bass.ds(h, 1)]
                    bias_q = bias[LOW, h:h + 1] if isinstance(h, int) else bias[LOW, bass.ds(h, 1)]
                    dve.wait_ge(act_split, (h * NC + what) * 2 + 1)
                    nc.vector.scalar_tensor_tensor(out=k_both[p][LOW, at], in0=src[TOP, :], scalar=bias_k,
                                                   in1=k_both[p][TOP, at].bitcast(F32),
                                                   op0=ALU.add, op1=ALU.subtract)
                    dve.wait_ge(act_split, (h * NC + (what + 1)) * 2)
                    nc.vector.scalar_tensor_tensor(out=q_lo[p][TOP, at], in0=src[LOW, :], scalar=bias_q,
                                                   in1=q_hi[p][LOW, at].bitcast(F32),
                                                   op0=ALU.add, op1=ALU.subtract)\
                        .then_inc(prep_freed[BANK[u]], 1)
                elif kind == "turn":
                    dve.wait_ge(prep_filled, h * UNITS + (u + 1))
                    nc.vector.tensor_tensor(q_lo[p][W:MR, what * C:(what + 1) * C].rearrange("r (j c) -> r j c", j=TC),
                                            src[0:TC, 0:P].unsqueeze(1).to_broadcast([TC, TC, P]), own_tile[:, :, :],
                                            ALU.mult).then_inc(prep_freed[BANK[u]], 1)
                else:
                    i, c = what
                    n = min(C, (i + 1) * P - c * C)
                    dve.wait_ge(prep_filled, h * UNITS + (u + 1))
                    nc.vector.tensor_reduce(part_max[:, i, c:c + 1], src[:, 0:n], AX_X, ALU.max)\
                        .then_inc(prep_freed[BANK[u]], 1)
                    if (i + 1) % TC == 0 and c == i // TC:
                        for b in range(2):
                            wait_freed(dve, h, max(v for v in range(u + 1) if BANK[v] == b and UNIT[v][0] == "maximum"))
                        if not (isinstance(h, int) and h == 0):
                            dve.wait_ge(prep_filled, (h - 1) * UNITS + (TURN[c] + 1))
                        tiles = slice(c * TC, (c + 1) * TC)
                        nc.vector.tensor_reduce(neg_max[:, tiles], part_max[:, tiles, 0:c + 1], AX_X, ALU.max,
                                                negate=True).then_inc(max_done, 1)

            def invert(h, qc):
                dve.wait_ge(sum_done, h * NC + (qc + 3))
                nc.vector.reciprocal(inv[:, :], sum_bank[:, 0:TC]).then_inc(inv_done, 1)

            def add(h, qc, j):
                t = qc * TC + j
                if j == 0:
                    dve.wait_ge(inv_done, h * NC + (qc + 2))
                    dve.wait_ge(mixed, h * NC + (qc + 2))
                last = nc.vector.scalar_tensor_tensor(out=attn[:, t, :], in0=out_bank[qc % 2][:, j * P:(j + 1) * P],
                                                      scalar=inv[:, j:j + 1], in1=attn[:, t, :],
                                                      op0=ALU.mult, op1=ALU.add)
                if j == TC - 1:
                    last.then_inc(added, 1)
                    if isinstance(h, int) and h == H - 1:
                        finish(qc)

            def finish(qc):
                at = slice(qc * TC, (qc + 1) * TC)
                dve.wait_ge(added, (H - 1) * NC + (qc + 3))
                link(nc.vector.tensor_tensor(attn[:, at, :], attn[:, at, :], sh.g[:, at, :], ALU.mult))
                nc.vector.tensor_tensor(attn[:, at, :], attn[:, at, :], sh.x[:, at, :], ALU.add)\
                    .then_inc(result_done, 1)

            for s in range(NPAIR * GAPS):
                if s % 2 == 0 and s < 4 * T:
                    bias_v(s // 2)
                for u in late_units[s]:
                    prepare_unit(0, 0, u)

            def body(h, p, more):
                for n in range(NPAIR):
                    for gap in range(GAPS):
                        if gap == GAPS - 1 and n in SUM_STEP:
                            invert(h, SUM_STEP.index(n))
                        if more:
                            for u in late_units[n * GAPS + gap]:
                                prepare_unit(h + 1, 1 - p, u)
                        if n in ADD_STEP and gap < TC:
                            add(h, ADD_STEP.index(n), gap)
                for j in range(TC):
                    add(h, NC - 1, j)

            heads(dve, body)


INPUTS = [
    "L0_attn_x", "L0_attn_w_qkv", "L0_attn_w_out", "L0_attn_b_out", "L0_attn_gamma", "L0_attn_beta",
    "L0_ffn_attention_mask", "L0_ffn_position_ids", "L0_ffn_router_w", "L0_ffn_router_b", "L0_ffn_wq", "L0_ffn_wk",
    "L0_ffn_wv", "L0_ffn_wo", "L0_ffn_w1", "L0_ffn_w2", "L0_ffn_ln1", "L0_ffn_ln2",
    "L1_attn_W_Q", "L1_attn_W_K", "L1_attn_W_V", "L1_attn_W_O", "L1_attn_b_Q", "L1_attn_b_K", "L1_attn_b_V",
    "L1_attn_b_O", "L1_ffn_w_gate", "L1_ffn_w_up", "L1_ffn_w_down",
]


def build(nc, a, out):
    with ExitStack() as ctx:
        sh = Shared()

        def sb(name, shape, dt=F32):
            return ctx.enter_context(nc.sbuf_tensor(name, shape, dt))

        sh.x = sb("x", [P, T, D])
        sh.xa = sb("xa", [P, T, D + 2])
        sh.xnT = sb("xnT", [P, S])
        sh.g = sb("g", [P, T, D])
        sh.ident = sb("ident", [P, P])
        sh.ones = sb("ones", [P, P])
        sh.psum = ctx.enter_context(nc.psum_tensor("psum", [P, 8, C], F32))
        sh.bank = [sh.psum[:, b, :] for b in range(8)]
        sh.parts_dram = nc.dram_tensor("parts_dram", [2, PARTS, D, S], BF16, kind="Internal").ap()
        with ExitStack() as layer0:
            sh.v0 = layer0.enter_context(nc.sbuf_tensor("v0", [P, T, D], F32))
            sh.o0 = layer0.enter_context(nc.sbuf_tensor("o0", [P, 1 + G * NC, TC, GH * HD0], F32))
            sh.q_rows = layer0.enter_context(nc.sbuf_tensor("q_rows0", [P, GH, S], BF16))
            sh.k_rows = layer0.enter_context(nc.sbuf_tensor("k_rows0", [P, GH, S], BF16))
            sh.v_cols = layer0.enter_context(nc.sbuf_tensor("v_cols0", [P, T, GH, VW], F32))
            sh.rows_loaded = layer0.enter_context(nc.semaphore("rows_loaded0"))
            prepare(nc, a, sh)
            routed0(nc, a, sh)
            attention0(nc, a, sh)
            join0(nc, a, sh)
        gated1(nc, a, sh)
        attention1(nc, a, sh, out)


def kernel(**inputs):
    import concourse.bacc as bacc
    from concourse.bass_utils import run_bass_kernel_spmd

    nc = bacc.Bacc("TRN2", target_bir_lowering=False, num_devices=1)
    arrays, a = {}, {}
    for name in INPUTS:
        array = np.ascontiguousarray(inputs[name])
        arrays["in_" + name] = array
        a[name] = nc.dram_tensor("in_" + name, array.shape, mybir.dt.from_np(array.dtype), kind="ExternalInput").ap()
    out = nc.dram_tensor("out", (1, S, D), F32, kind="ExternalOutput").ap()
    build(nc, a, out)
    result = run_bass_kernel_spmd(nc, [arrays], core_ids=[0])
    return result.results[0]["out"]
```
